# Optimizing a Trainium2 kernel written in Bass

```python
import numpy as np
import jax
import jax.numpy as jnp

def _softmax(x, axis=-1):
    return jax.nn.softmax(x, axis=axis)

def _gelu(x):
    return jax.nn.gelu(x, approximate=True)

def _silu(x):
    return jax.nn.silu(x)

def _sigmoid(x):
    return jax.nn.sigmoid(x)

def _layernorm(x, axis=-1, eps=1e-05):
    m = jnp.mean(x, axis=axis, keepdims=True)
    v = jnp.var(x, axis=axis, keepdims=True)
    return (x - m) / jnp.sqrt(v + eps)

def _scatter_add(tgt, idx, src, axis=0):
    return tgt.at[idx].add(src)

def _segment_sum(src, seg, n):
    return jax.ops.segment_sum(src, seg, n)
kernel_name = 'mk_conv_attn_hybrid_d2_conv_nchw512_r4_3dd836'

def setup_inputs(seed: int=0):
    np.random.seed(seed)
    _w = jnp.asarray

    def _rec_inputs():
        import jax
        import jax.numpy as jnp
        _gk = jax.random.key(seed)
        x = -0.0002928 + 1 * jax.random.normal(jax.random.fold_in(_gk, 1), (8, 128, 32, 32), jnp.float32)
        return x
    x = _rec_inputs()

    def _L0_conv_setup():
        import jax, jax.numpy as jnp
        import numpy as np
        import math
        B, C, H, W = (8, 128, 32, 32)
        NH = 8
        G = 32
        EPS = 1e-06

        def group_norm(x, gamma, beta, groups=G, eps=EPS):
            b, c, h, w = x.shape
            xr = x.reshape(b, groups, c // groups, h, w)
            mu = xr.mean(axis=(2, 3, 4), keepdims=True)
            var = xr.var(axis=(2, 3, 4), keepdims=True)
            xn = ((xr - mu) * jax.lax.rsqrt(var + eps)).reshape(b, c, h, w)
            return xn * gamma[None, :, None, None] + beta[None, :, None, None]

        def conv2d(x, w, b, pad):
            y = jax.lax.conv_general_dilated(x, w, window_strides=(1, 1), padding=[(pad, pad), (pad, pad)], dimension_numbers=('NCHW', 'OIHW', 'NCHW'))
            return y + b[None, :, None, None]
        key = jax.random.key(seed)
        ks = jax.random.split(key, 20)

        def n(k, shape, s=0.02):
            return jax.random.normal(k, shape, dtype=jnp.float32) * s
        f32 = jnp.float32
        return {'hidden_states': jax.random.normal(ks[0], (B, C, H, W), dtype=f32), 'pre_g': jnp.ones(C, f32), 'pre_b': jnp.zeros(C, f32), 'norm_g': jnp.ones(C, f32), 'norm_b': jnp.zeros(C, f32), 'post_g': jnp.ones(C, f32), 'post_b': jnp.zeros(C, f32), 'pos_emb': n(ks[1], (1, C, 32, 32)), 'wq': n(ks[2], (C, C)), 'wk': n(ks[3], (C, C)), 'wv': n(ks[4], (C, C)), 'wq0': n(ks[5], (C // 2, C)), 'wq1': n(ks[6], (C // 2, C)), 'wk0': n(ks[7], (C // 2, C)), 'wk1': n(ks[8], (C // 2, C)), 'wv0': n(ks[9], (C // 2, C)), 'wv1': n(ks[10], (C // 2, C)), 'sa_w1': n(ks[11], (C // 8, C, 1, 1)), 'sa_b1': jnp.zeros(C // 8, f32), 'sa_w2': n(ks[12], (C // 8, C // 8, 3, 3)), 'sa_b2': jnp.zeros(C // 8, f32), 'sa_w3': n(ks[13], (1, C // 8, 1, 1)), 'sa_b3': jnp.zeros(1, f32), 'ff_w1': n(ks[14], (C, 2 * C)), 'ff_b1': jnp.zeros(C, f32), 'ff_w2': n(ks[15], (C, C)), 'ff_b2': jnp.zeros(C, f32), 'out_w': n(ks[16], (C, C)), 'out_b': jnp.zeros(C, f32)}
    _L0_conv_all = _L0_conv_setup()
    _L0_conv_in = {k: v for k, v in _L0_conv_all.items() if k in ('pre_g', 'pre_b', 'norm_g', 'norm_b', 'post_g', 'post_b', 'pos_emb', 'wq', 'wk', 'wv', 'wq0', 'wq1', 'wk0', 'wk1', 'wv0', 'wv1', 'sa_w1', 'sa_b1', 'sa_w2', 'sa_b2', 'sa_w3', 'sa_b3', 'ff_w1', 'ff_b1', 'ff_w2', 'ff_b2', 'out_w', 'out_b')}
    del _L0_conv_all

    def _L1_attn_setup():
        import jax, jax.numpy as jnp
        import numpy as np
        NUM_HEADS = 8
        SCALE = 16 ** (-0.5)
        key = jax.random.key(seed)
        k1, k2 = jax.random.split(key)
        B, S, D = (4, 512, 128)
        x = jax.random.normal(k1, (B, S, D), dtype=jnp.float32)
        w_qkv = jax.random.normal(k2, (D, 3 * D), dtype=jnp.float32) * D ** (-0.5)
        return {'x': x, 'w_qkv': w_qkv}
    _L1_attn_all = _L1_attn_setup()
    _L1_attn_in = {k: v for k, v in _L1_attn_all.items() if k in ('w_qkv',)}
    del _L1_attn_all

    def _L1_ffn_setup():
        import jax, jax.numpy as jnp
        import numpy as np
        TOP_K = 2
        key = jax.random.key(seed)
        ks = jax.random.split(key, 4)
        B, S, D, H, E = (2, 1024, 128, 512, 8)
        scale_in = 1.0 / np.sqrt(D)
        scale_h = 1.0 / np.sqrt(H)
        return {'x': jax.random.normal(ks[0], (B, S, D), dtype=jnp.float32), 'gate_w': jax.random.normal(ks[1], (D, E), dtype=jnp.float32) * scale_in, 'gate_b': jnp.zeros((E,), dtype=jnp.float32), 'w1': jax.random.normal(ks[2], (E, D, H), dtype=jnp.float32) * scale_in, 'b1': jnp.zeros((E, H), dtype=jnp.float32), 'w2': jax.random.normal(ks[3], (E, H, D), dtype=jnp.float32) * scale_h, 'b2': jnp.zeros((E, D), dtype=jnp.float32)}
    _L1_ffn_all = _L1_ffn_setup()
    _L1_ffn_in = {k: v for k, v in _L1_ffn_all.items() if k in ('gate_w', 'gate_b', 'w1', 'b1', 'w2', 'b2')}
    del _L1_ffn_all
    return {'x': x, 'L0_conv_pre_g': _L0_conv_in['pre_g'], 'L0_conv_pre_b': _L0_conv_in['pre_b'], 'L0_conv_norm_g': _L0_conv_in['norm_g'], 'L0_conv_norm_b': _L0_conv_in['norm_b'], 'L0_conv_post_g': _L0_conv_in['post_g'], 'L0_conv_post_b': _L0_conv_in['post_b'], 'L0_conv_pos_emb': _L0_conv_in['pos_emb'], 'L0_conv_wq': _L0_conv_in['wq'], 'L0_conv_wk': _L0_conv_in['wk'], 'L0_conv_wv': _L0_conv_in['wv'], 'L0_conv_wq0': _L0_conv_in['wq0'], 'L0_conv_wq1': _L0_conv_in['wq1'], 'L0_conv_wk0': _L0_conv_in['wk0'], 'L0_conv_wk1': _L0_conv_in['wk1'], 'L0_conv_wv0': _L0_conv_in['wv0'], 'L0_conv_wv1': _L0_conv_in['wv1'], 'L0_conv_sa_w1': _L0_conv_in['sa_w1'], 'L0_conv_sa_b1': _L0_conv_in['sa_b1'], 'L0_conv_sa_w2': _L0_conv_in['sa_w2'], 'L0_conv_sa_b2': _L0_conv_in['sa_b2'], 'L0_conv_sa_w3': _L0_conv_in['sa_w3'], 'L0_conv_sa_b3': _L0_conv_in['sa_b3'], 'L0_conv_ff_w1': _L0_conv_in['ff_w1'], 'L0_conv_ff_b1': _L0_conv_in['ff_b1'], 'L0_conv_ff_w2': _L0_conv_in['ff_w2'], 'L0_conv_ff_b2': _L0_conv_in['ff_b2'], 'L0_conv_out_w': _L0_conv_in['out_w'], 'L0_conv_out_b': _L0_conv_in['out_b'], 'L1_attn_w_qkv': _L1_attn_in['w_qkv'], 'L1_ffn_gate_w': _L1_ffn_in['gate_w'], 'L1_ffn_gate_b': _L1_ffn_in['gate_b'], 'L1_ffn_w1': _L1_ffn_in['w1'], 'L1_ffn_b1': _L1_ffn_in['b1'], 'L1_ffn_w2': _L1_ffn_in['w2'], 'L1_ffn_b2': _L1_ffn_in['b2']}

def reference(x, L0_conv_pre_g, L0_conv_pre_b, L0_conv_norm_g, L0_conv_norm_b, L0_conv_post_g, L0_conv_post_b, L0_conv_pos_emb, L0_conv_wq, L0_conv_wk, L0_conv_wv, L0_conv_wq0, L0_conv_wq1, L0_conv_wk0, L0_conv_wk1, L0_conv_wv0, L0_conv_wv1, L0_conv_sa_w1, L0_conv_sa_b1, L0_conv_sa_w2, L0_conv_sa_b2, L0_conv_sa_w3, L0_conv_sa_b3, L0_conv_ff_w1, L0_conv_ff_b1, L0_conv_ff_w2, L0_conv_ff_b2, L0_conv_out_w, L0_conv_out_b, L1_attn_w_qkv, L1_ffn_gate_w, L1_ffn_gate_b, L1_ffn_w1, L1_ffn_b1, L1_ffn_w2, L1_ffn_b2):
    import jax
    import jax.numpy as jnp

    def _L0_conv_ref(hidden_states, pre_g, pre_b, norm_g, norm_b, post_g, post_b, pos_emb, wq, wk, wv, wq0, wq1, wk0, wk1, wv0, wv1, sa_w1, sa_b1, sa_w2, sa_b2, sa_w3, sa_b3, ff_w1, ff_b1, ff_w2, ff_b2, out_w, out_b):
        import jax, jax.numpy as jnp
        import numpy as np
        import math
        B, C, H, W = (8, 128, 32, 32)
        NH = 8
        G = 32
        EPS = 1e-06

        def group_norm(x, gamma, beta, groups=G, eps=EPS):
            b, c, h, w = x.shape
            xr = x.reshape(b, groups, c // groups, h, w)
            mu = xr.mean(axis=(2, 3, 4), keepdims=True)
            var = xr.var(axis=(2, 3, 4), keepdims=True)
            xn = ((xr - mu) * jax.lax.rsqrt(var + eps)).reshape(b, c, h, w)
            return xn * gamma[None, :, None, None] + beta[None, :, None, None]

        def conv2d(x, w, b, pad):
            y = jax.lax.conv_general_dilated(x, w, window_strides=(1, 1), padding=[(pad, pad), (pad, pad)], dimension_numbers=('NCHW', 'OIHW', 'NCHW'))
            return y + b[None, :, None, None]
        b, c, h, w = hidden_states.shape
        S = h * w
        residual = hidden_states
        x = group_norm(hidden_states, pre_g, pre_b)
        x = x + pos_emb
        s1 = jax.nn.silu(conv2d(x, sa_w1, sa_b1, 0))
        s2 = jax.nn.silu(conv2d(s1, sa_w2, sa_b2, 1))
        spatial_weights = jax.nn.sigmoid(conv2d(s2, sa_w3, sa_b3, 0))
        spatial_enhanced = x * spatial_weights
        sh = group_norm(x, norm_g, norm_b).reshape(b, c, S).transpose(0, 2, 1)
        enc = sh
        hd = c // NH

        def split_heads(t):
            return t.reshape(b, S, NH, hd).transpose(0, 2, 1, 3)
        qh = split_heads(sh @ wq.T)
        kh = split_heads(enc @ wk.T)
        vh = split_heads(enc @ wv.T)
        scores = jnp.einsum('bhqd,bhkd->bhqk', qh, kh) / math.sqrt(hd)
        probs = jax.nn.softmax(scores, axis=-1)
        standard_out = jnp.einsum('bhqk,bhkd->bhqd', probs, vh)
        standard_out = standard_out.transpose(0, 2, 1, 3).reshape(b, S, c)
        msh = spatial_enhanced.reshape(b, c, S).transpose(0, 2, 1)
        parts = []
        for wqm, wkm, wvm in ((wq0, wk0, wv0), (wq1, wk1, wv1)):
            qm = msh @ wqm.T
            km = enc @ wkm.T
            vm = enc @ wvm.T
            sc = jnp.einsum('bqd,bkd->bqk', qm, km) / math.sqrt(qm.shape[-1])
            parts.append(jnp.einsum('bqk,bkd->bqd', jax.nn.softmax(sc, axis=-1), vm))
        multi_out = jnp.concatenate(parts, axis=-1)
        combined = jnp.concatenate([standard_out, multi_out], axis=-1)
        fused = jax.nn.silu(combined @ ff_w1.T + ff_b1) @ ff_w2.T + ff_b2
        final = fused @ out_w.T + out_b
        final = final.transpose(0, 2, 1).reshape(b, c, h, w)
        final = group_norm(final, post_g, post_b)
        return final + residual

    def _L1_attn_ref(x, w_qkv):
        import jax, jax.numpy as jnp
        import numpy as np
        NUM_HEADS = 8
        SCALE = 16 ** (-0.5)
        B, S, D = x.shape
        H = NUM_HEADS
        Dh = D // H
        qkv = x @ w_qkv
        q, k, v = jnp.split(qkv, 3, axis=-1)

        def heads(t):
            return t.reshape(B, S, H, Dh).transpose(0, 2, 1, 3)
        q, k, v = (heads(q), heads(k), heads(v))
        dots = jnp.einsum('bhqd,bhkd->bhqk', q, k) * SCALE
        attn = jax.nn.softmax(dots, axis=-1)
        out = jnp.einsum('bhqk,bhkd->bhqd', attn, v)
        return out.transpose(0, 2, 1, 3).reshape(B, S, D)

    def _L1_ffn_ref(x, gate_w, gate_b, w1, b1, w2, b2):
        import jax, jax.numpy as jnp
        import numpy as np
        TOP_K = 2
        B, S, D = x.shape
        E = gate_w.shape[1]
        flat_x = x.reshape(-1, D)
        gate_logits = flat_x @ gate_w + gate_b
        raw_weights = jax.nn.softmax(gate_logits, axis=-1)
        top_w, top_idx = jax.lax.top_k(raw_weights, TOP_K)
        one_hot = jax.nn.one_hot(top_idx, E, dtype=flat_x.dtype)
        gate_output = (one_hot * top_w[..., None]).sum(axis=-2)
        h = jax.nn.gelu(jnp.einsum('td,edh->teh', flat_x, w1) + b1, approximate=False)
        expert_out = jnp.einsum('teh,ehd->ted', h, w2) + b2
        combined = jnp.einsum('ted,te->td', expert_out, gate_output)
        return combined.reshape(B, S, -1)

    def _gn(v, G=32, eps=1e-05):
        B_, C_, H_, W_ = v.shape
        g = v.reshape(B_, G, C_ // G, H_, W_)
        m = jnp.mean(g, axis=(2, 3, 4), keepdims=True)
        s = jnp.var(g, axis=(2, 3, 4), keepdims=True)
        return ((g - m) / jnp.sqrt(s + eps)).reshape(v.shape)

    def _ln_c(v, eps=1e-06):
        m = jnp.mean(v, axis=1, keepdims=True)
        s = jnp.var(v, axis=1, keepdims=True)
        return (v - m) / jnp.sqrt(s + eps)

    def _ln_t(v, eps=1e-05):
        m = jnp.mean(v, axis=-1, keepdims=True)
        s = jnp.var(v, axis=-1, keepdims=True)
        return (v - m) / jnp.sqrt(s + eps)

    def _to_tokens(v):
        B_, C_, H_, W_ = v.shape
        return v.reshape(B_, C_, H_ * W_).transpose(0, 2, 1)

    def _from_tokens(t, like):
        B_, C_, H_, W_ = like.shape
        return t.transpose(0, 2, 1).reshape(B_, C_, H_, W_)
    x = _L0_conv_ref(x, L0_conv_pre_g, L0_conv_pre_b, L0_conv_norm_g, L0_conv_norm_b, L0_conv_post_g, L0_conv_post_b, L0_conv_pos_emb, L0_conv_wq, L0_conv_wk, L0_conv_wv, L0_conv_wq0, L0_conv_wq1, L0_conv_wk0, L0_conv_wk1, L0_conv_wv0, L0_conv_wv1, L0_conv_sa_w1, L0_conv_sa_b1, L0_conv_sa_w2, L0_conv_sa_b2, L0_conv_sa_w3, L0_conv_sa_b3, L0_conv_ff_w1, L0_conv_ff_b1, L0_conv_ff_w2, L0_conv_ff_b2, L0_conv_out_w, L0_conv_out_b)
    t = _to_tokens(x)
    t = t + _L1_attn_ref(_ln_t(t), L1_attn_w_qkv)
    t = t + _L1_ffn_ref(_ln_t(t), L1_ffn_gate_w, L1_ffn_gate_b, L1_ffn_w1, L1_ffn_b1, L1_ffn_w2, L1_ffn_b2)
    x = _from_tokens(t, x)
    return x

_drawn_inputs = setup_inputs


def setup_inputs(seed=0):
    import zlib

    import numpy as np

    out = dict(_drawn_inputs(seed))
    spreads = {'L0_conv_pre_g': (1.0, 0.6),
     'L0_conv_pre_b': (0.0, 0.8),
     'L0_conv_norm_g': (1.0, 0.6),
     'L0_conv_norm_b': (0.0, 0.8),
     'L0_conv_post_g': (1.0, 0.2),
     'L0_conv_post_b': (0.0, 0.1),
     'L0_conv_sa_b1': (0.0, 0.8),
     'L0_conv_sa_b2': (0.0, 2.0),
     'L0_conv_ff_b1': (0.0, 0.459),
     'L0_conv_ff_b2': (0.0, 0.1),
     'L0_conv_out_b': (0.0, 0.1),
     'L1_ffn_gate_b': (0.0, 0.276),
     'L1_ffn_b1': (0.0, 0.509),
     'L1_ffn_b2': (0.0, 0.325)}
    factors = {'L0_conv_pos_emb': 8.0,
     'L0_conv_wq': 8.0,
     'L0_conv_wk': 8.0,
     'L0_conv_wv': 8.0,
     'L0_conv_wq0': 8.0,
     'L0_conv_wq1': 8.0,
     'L0_conv_wk0': 8.0,
     'L0_conv_wk1': 8.0,
     'L0_conv_wv0': 8.0,
     'L0_conv_wv1': 8.0,
     'L0_conv_sa_w1': 8.0,
     'L0_conv_sa_w2': 8.0,
     'L0_conv_sa_w3': 8.0,
     'L0_conv_ff_w1': 7.648}
    for name, (base, spread) in spreads.items():
        noise = np.random.default_rng([zlib.crc32(name.encode()), seed]).standard_normal(out[name].shape)
        drawn = base * np.exp(spread * noise) if base else spread * noise
        out[name] = jnp.asarray(drawn.astype(out[name].dtype))
    for name, factor in factors.items():
        out[name] = (out[name] * factor).astype(out[name].dtype)
    return out
```

```python
from contextlib import ExitStack

import concourse.bass as bass
from concourse import mybir

F32 = mybir.dt.float32
BF16 = mybir.dt.bfloat16
U32 = mybir.dt.uint32
ACT = mybir.ActivationFunctionType
ALU = mybir.AluOpType
AX = mybir.AxisListType

P = 128
S = 1024
HALF = 512
NT = S // P
NH = 8
HD = P // NH
NG = 2
PIECES = 6
K_PARTS = (0, 1, 0, 1, 2, 0)
Q_PARTS = (0, 0, 1, 1, 0, 2)
ROWS = PIECES * HD
NE = 8
HID = 512
NC = HID // P
SIDE = 32
MULTI = 2
MD = 64
STEPS = 16

SC = 0
OB = 4
MX = 5
GL = 7

WEIGHTS = ["wk", "wq", "wv", "wkB", "wqB", "wvB", "ffa0", "ffa1", "ffb", "ff2", "out",
           "wvm", "wkm0", "wkm1", "wqm0", "wqm1", "ident", "group", "spread_sum", "ones"]
VECTORS = ["pre_g", "pre_b", "norm_g", "norm_b", "post_g", "post_b", "ff_b1", "ff_b2", "out_b",
           "sa_b1", "sa_b2", "sa_b3", "neg_half"]


class Steps:

    def __init__(self, *names):
        self.names, self.done = names, 0

    def __getitem__(self, name):
        return self.names.index(name) + 1

    def one(self, name):
        assert self.names[self.done] == name, (name, self.names[self.done])
        self.done += 1
        return 1


class Turns:

    def __init__(self):
        self.n = 0

    def next(self):
        self.n += 1
        return self.n


def max_blocks(attn):
    units = NH + (MULTI if attn == 0 else 0)
    return [(u, t, k) for u in range(units) for t in range(NT) for k in range(2)]


def max_plan(attn, n):
    if n < STEPS:
        return range(64 + 5 * n, min(64 + 5 * n + 5, 128)), {4: 4, 7: 5, 10: 6, 13: 7}.get(n)
    s = n - STEPS
    if attn == 0 and s < STEPS:
        return range(128 + 3 * s, min(128 + 3 * s + 3, 160)), {7: 8, 12: 9}.get(s)
    return range(0), None


def build(nc, x, pos, wts, vecs, sa1, sa2, sa3, w1, b1, w2, b2, gw, gb, iota, out):
    NB = x.shape[0]
    ctx = ExitStack()
    with ctx:
        def sb(name, shape, dt=F32):
            return ctx.enter_context(nc.sbuf_tensor(name, shape, dt))

        def sem(name):
            return ctx.enter_context(nc.semaphore(name))

        ps = ctx.enter_context(nc.psum_tensor("ps", [P, 8, HALF], F32))

        wt = sb("wt", [P, len(WEIGHTS), P])
        vec = sb("vec", [P, len(VECTORS)])
        half_b = sb("half_b", [P, 4])
        posw = sb("posw", [P, S])
        sa1w = sb("sa1w", [P, 96])
        sa2w = sb("sa2w", [96, 3, HD])
        sa3w = sb("sa3w", [HD, P])
        w1w = sb("w1w", [P, NE, HID])
        w2w = sb("w2w", [P, NE, NC, P])
        b1w = sb("b1w", [P, NE, NC])
        b2w = sb("b2w", [NE, P])
        gww = sb("gww", [P, NE])
        gbw = sb("gbw", [P, NT, NE])
        iow = sb("iow", [P, NT, NE])

        def w(name):
            return wt[:, WEIGHTS.index(name), :]

        def v(name, n=P):
            i = VECTORS.index(name)
            return vec[0:n, i:i + 1]

        xin = sb("xin", [P, S])
        x1 = sb("x1", [P, S])
        xh = sb("xh", [P, S])
        gated = sb("gated", [P, S])
        ta = sb("ta", [P, S])
        tb = sb("tb", [P, S])
        conv_in = sb("conv_in", [96, SIDE + 2, SIDE])
        conv2 = sb("conv2", [HD, S])
        parts = sb("parts", [P, 2, 3, S], BF16)
        ks = sb("ks", [ROWS + 3, NH, S], BF16)
        qs = sb("qs", [ROWS + 3, NH, S], BF16)
        va = sb("va", [P, NT, NH, 2 * HD])
        vm = sb("vm", [P, NT, P])
        km = sb("km", [MD + 1, MULTI, S])
        qm = sb("qm", [MD + 1, MULTI, S])
        kmh = sb("kmh", [P, MULTI, S], BF16)
        qmh = sb("qmh", [P, MULTI, S], BF16)
        prob = sb("prob", [P, 3, 4, HALF])
        oatt = sb("oatt", [P, 4, HALF])
        rec = tb[:, HALF:S]
        omul = gated
        tok = sb("tok", [P, NT, P])
        blockmax = sb("blockmax", [P, 10, NT, 2])
        negmax = sb("negmax", [P, 10, NT])
        maxrow = sb("maxrow", [NT, NH, 3, P], BF16)
        maxrow_m = sb("maxrow_m", [NT, MULTI, P])
        st = sb("st", [P, NT, 6])
        mv = sb("mv", [P, NT, 2])
        gs = sb("gs", [P, 2])
        vn = sb("vn", [P, NT])
        rs = sb("rs", [P, NT])
        nb = sb("nb", [P, NT])
        ca = sb("ca", [P, 1])
        cb = sb("cb", [P, 1])
        logit = sb("logit", [P, NT, NE])
        top = sb("top", [P, NT, 8])
        topi = sb("topi", [P, NT, 8], U32)
        topf = sb("topf", [P, NT, 2])
        ex = sb("ex", [P, NT, NE])
        oh = sb("oh", [P, NT, NE])
        gate = sb("gate", [P, NT, NE])
        esum = sb("esum", [P, NT])
        erec = sb("erec", [P, NT])
        gate_t = conv2[0:NE, :]

        rem = [prob[:, 2, 0:2, :].rearrange("p a s -> p (a s)"),
               prob[:, 2, 2:4, :].rearrange("p a s -> p (a s)")]
        hid = prob
        lnt = ta[:, :].rearrange("p (t c) -> p t c", t=NT)

        parts_dram = nc.dram_tensor("parts_dram", (2, P, 3, S), BF16, kind="Internal").ap()
        maxrow_dram = nc.dram_tensor("maxrow_dram", (NH, NT, 3, P), BF16, kind="Internal").ap()
        maxrow_m_dram = nc.dram_tensor("maxrow_m_dram", (MULTI, NT, P), F32, kind="Internal").ap()

        weights_in, consts_set = sem("weights_in"), sem("consts_set")

        first = sem("x_in")
        x_in = first
        pe_done, act_done, dve_done, pool_done = sem("pe_done"), sem("act_done"), sem("dve_done"), sem("pool_done")
        dve_chain = sem("dve_chain")
        small_full, small_free = sem("small_full"), sem("small_free")
        parts_out = [sem("parts_out_a"), sem("parts_out_b")]
        spread = [sem("spread_a"), sem("spread_b")]
        blocks_ready = [sem("blocks_ready_a"), sem("blocks_ready_b")]
        blocks_used = [sem("blocks_used_a"), sem("blocks_used_b")]
        max_ready = [sem("max_ready_a"), sem("max_ready_b")]
        rows_split = [sem("rows_split_a"), sem("rows_split_b")]
        rows_out = [sem("rows_out_a"), sem("rows_out_b")]
        rows_in = [sem("rows_in_a"), sem("rows_in_b")]
        scores_ready = [sem("scores_ready_a"), sem("scores_ready_b")]
        exp_done = [sem("exp_done_a"), sem("exp_done_b")]
        pv_done = [sem("pv_done_a"), sem("pv_done_b")]
        o_taken = [sem("o_taken_a"), sem("o_taken_b")]
        o_scaled = [sem("o_scaled_a"), sem("o_scaled_b")]
        ms_ready, mexp_done, mpv_done, mo_taken, mo_scaled = (
            sem("ms_ready"), sem("mexp_done"), sem("mpv_done"), sem("mo_taken"), sem("mo_scaled"))
        hid_ready, gelu_done, y_ready, y_used = sem("hid_ready"), sem("gelu_done"), sem("y_ready"), sem("y_used")
        out_done = sem("out_done")
        cleared = range(first.num, out_done.num + 1)

        with nc.Block() as block:
            @block.sync
            def _(sp):
                for dst, src in ((wt[:, :, :], wts), (vec[:, :], vecs), (posw[:, :], pos), (sa1w[:, :], sa1),
                                 (sa2w[:, :, :], sa2), (sa3w[:, :], sa3), (w1w[:, :, :], w1),
                                 (w2w[:, :, :, :], w2), (b1w[:, :, :], b1), (b2w[:, :], b2), (gww[:, :], gw),
                                 (gbw[:, :, :], gb), (iow[:, :, :], iota)):
                    sp.dma_start(dst, src).then_inc(weights_in, 16)
                sp.wait_ge(weights_in, 16 * 13)

            @block.vector
            def _(dve):
                dve.memset(conv_in[:, :, :], 0.0).then_inc(consts_set, 1)
                dve.memset(ks[ROWS:ROWS + 3, :, :], 1.0).then_inc(consts_set, 1)
                dve.memset(va[:, :, :, :], 1.0).then_inc(consts_set, 1)
                dve.memset(km[MD:MD + 1, :, :], 1.0).then_inc(consts_set, 1)
                dve.wait_ge(weights_in, 16 * 13)
                for i, name in enumerate(("ff_b1", "sa_b1", "sa_b2", "sa_b3")):
                    dve.tensor_scalar(half_b[:, i:i + 1], v(name), 0.5, None, ALU.mult).then_inc(consts_set, 1)
                dve.wait_ge(consts_set, 8)

        PE = Steps("conv1", "k_a", "q_a", "conv2", "conv3", "v_a", "vm", "km", "qm", "ff1", "ff2", "outp",
                   "tr_x", "tr_n_b", "k_b", "q_b", "v_b", "tr_o", "tr_n_e", "tr_g", "b2", "tr_out")
        AC = Steps("tanh1", "k1_a", "q1_a", "k2_a", "q2_a", "tanh2", "tanh3", "vm", "km", "qm", "tanh_ff", "ff2",
                   "outp", "tok", "xh_b", "k1_b", "q1_b", "k2_b", "q2_b", "xh_e", "gate_exp", "result")
        DV = Steps("pre_stats", "pre_var", "x1", "norm_stats", "norm_var", "xh_a", "u1", "conv_in", "k_rem_a", "q_rem_a", "k3_a", "q3_a", "u2", "conv2",
                   "v_a", "gated", "kmh", "qmh", "ff_act", "post_stats", "post_var", "xr", "ln_var_b", "ln_b",
                   "k_rem_b", "q_rem_b", "k3_b", "q3_b", "v_b", "tok2", "ln_var_e", "ln_e",
                   "gate_diff", "gates", "gate_t", "b2")
        PL = Steps("pre_rstd", "norm_rstd", "post_rstd", "ln_rstd_b", "ln_rstd_e")
        AB = "ab"

        def halves(first_bank, rows=P):
            return ps[0:rows, first_bank:first_bank + 2, :]

        def two(ap):
            return ap.rearrange("p (a s) -> p a s", a=2)

        with nc.Fori(0, NB) as img:
            with nc.Block(no_gpsimd_drain=True) as block:

                @block.sync
                def _(sp):
                    sp.dma_start(xin[:, :], x[bass.ds(img, 1)].rearrange("a p s -> (a p) s")).then_inc(x_in, 16)

                    def spread_parts(a):
                        for i, (t, pieces, dst) in enumerate((("k3", K_PARTS, ks), ("q3", Q_PARTS, qs))):
                            sp.wait_ge(dve_done, DV[f"{t}_{AB[a]}"])
                            sp.dma_start(parts_dram[i], parts[:, i, :, :]).then_inc(parts_out[a], 16)
                            sp.wait_ge(parts_out[a], 16 * (i + 1))
                            for j, part in enumerate(pieces):
                                sp.dma_start(dst[HD * j:HD * (j + 1), :, :],
                                             parts_dram[i, :, part, :].rearrange("(h d) s -> d h s", d=HD)
                                             ).then_inc(spread[a], 16)

                    def spread_max(a, u, n):
                        sp.wait_ge(rows_split[a], n)
                        if u < NH:
                            sp.dma_start(maxrow_dram[u], maxrow[:, u, :, :]).then_inc(rows_out[a], 16)
                            sp.wait_ge(rows_out[a], 16 * n)
                            sp.dma_start(qs[ROWS:ROWS + 3, u, :].rearrange("r (t s) -> r t s", t=NT),
                                         maxrow_dram[u].rearrange("t r s -> r t s")).then_inc(rows_in[a], 16)
                        else:
                            m = u - NH
                            sp.dma_start(maxrow_m_dram[m], maxrow_m[:, m, :]).then_inc(rows_out[a], 16)
                            sp.wait_ge(rows_out[a], 16 * n)
                            sp.dma_start(qm[MD:MD + 1, m, :],
                                         maxrow_m_dram[m:m + 1].rearrange("m t s -> m (t s)")).then_inc(rows_in[a], 16)

                    for a in range(2):
                        spread_parts(a)
                        for u in range(NH + (MULTI if a == 0 else 0)):
                            spread_max(a, u, u + 1)
                    sp.wait_ge(act_done, AC["result"])
                    sp.dma_start(out[bass.ds(img, 1)].rearrange("a p s -> (a p) s"), tb[:, :]).then_inc(out_done, 16)
                    sp.wait_ge(out_done, 16)
                    sp.wait_ge(rows_in[1], 16 * NH)

                @block.gpsimd
                def _(pool):
                    for var, name, n in (("pre_var", "pre_rstd", 1), ("norm_var", "norm_rstd", 1), ("post_var", "post_rstd", 1),
                                         ("ln_var_b", "ln_rstd_b", NT), ("ln_var_e", "ln_rstd_e", NT)):
                        pool.wait_ge(dve_done, DV[var])
                        pool.tensor_tensor(rs[:, 0:n], vn[:, 0:n], v("neg_half").to_broadcast([P, n]),
                                           ALU.pow).then_inc(pool_done, PL.one(name))

                @block.tensor
                def _(pe):
                    small = Turns()

                    def small_turn():
                        k = small.next()
                        if k > 1:
                            pe.wait_ge(small_free, k - 1)

                    def group_stats(name):
                        small_turn()
                        pe.wait_ge(dve_done, DV[f"{name}_stats"])
                        pe.matmul(ps[:, GL, 0:2], w("group"), mv[:, 0, :], start=True, stop=True).then_inc(small_full, 1)

                    def project(bank, weight, src, name, m=P):
                        for h in range(2):
                            mm = pe.matmul(ps[0:m, bank + h, :], weight, src[:, h * HALF:(h + 1) * HALF],
                                           start=True, stop=True)
                        mm.then_inc(pe_done, PE.one(name))

                    def values(bank, weight, name):
                        for t in range(NT):
                            mm = pe.matmul(ps[:, bank + t // 4, (t % 4) * P:(t % 4 + 1) * P], xh[:, t * P:(t + 1) * P],
                                           weight, start=True, stop=True)
                        mm.then_inc(pe_done, PE.one(name))

                    def transposes(bank, src, name, n=P):
                        for t in range(NT):
                            mm = pe.transpose(ps[0:n, bank + t // 4, (t % 4) * P:(t % 4 + 1) * P], src(t), w("ident"))
                        mm.then_inc(pe_done, PE.one(name))

                    def max_block(a, j):
                        u, t, k = max_blocks(a)[j]
                        if j >= 2:
                            pe.wait_ge(blocks_used[a], j - 1)
                        if u < NH:
                            lhs, rhs = qs[0:ROWS, u, t * P:(t + 1) * P], ks[0:ROWS, u, k * HALF:(k + 1) * HALF]
                        else:
                            lhs, rhs = qmh[:, u - NH, t * P:(t + 1) * P], kmh[:, u - NH, k * HALF:(k + 1) * HALF]
                        pe.matmul(ps[:, MX + j % 2, :], lhs, rhs, start=True, stop=True).then_inc(blocks_ready[a], 1)

                    def turn_max(a, u):
                        small_turn()
                        pe.wait_ge(max_ready[a], u + 1)
                        pe.transpose(ps[0:NT, GL, 0:P], negmax[:, u, :], w("ident")).then_inc(small_full, 1)

                    def scores(a, n):
                        g, q, t = n // STEPS, n // NT % 2, n % NT
                        if n % STEPS == 0:
                            pe.wait_ge(rows_in[a], 16 * 4 * (g + 1))
                        for pair in range(2):
                            if n >= 1:
                                pe.wait_ge(exp_done[a], 2 * (n - 1) + pair + 1)
                            for j in range(2):
                                h = 4 * g + 2 * pair + j
                                mm = pe.matmul(ps[:, SC + 2 * pair + j, :], ks[:, h, t * P:(t + 1) * P],
                                               qs[:, h, q * HALF:(q + 1) * HALF], start=True, stop=True)
                            mm.then_inc(scores_ready[a], 1)

                    def weigh_values(a, n):
                        g, t = n // STEPS, n % NT
                        pe.wait_ge(exp_done[a], 2 * n + 2)
                        if t == 0 and n:
                            pe.wait_ge(o_taken[a], n // NT)
                        for j in range(4):
                            mm = pe.matmul(ps[32 * j:32 * j + 32, OB, :], va[:, t, 4 * g + j, :], prob[:, n % 3, j, :],
                                           start=(t == 0), stop=(t == NT - 1))
                        mm.then_inc(pv_done[a], 1)

                    def sum_rows(a, f):
                        small_turn()
                        pe.wait_ge(o_taken[a], f + 1)
                        pe.matmul(ps[:, GL, :], w("spread_sum"), oatt[:, f, :], start=True, stop=True).then_inc(small_full, 1)

                    def attention(a):
                        pe.wait_ge(spread[a], 16 * 2 * PIECES)
                        for j in range(64):
                            max_block(a, j)
                            if j % 16 == 8 and j > 16:
                                turn_max(a, j // 16 - 1)
                        turn_max(a, 3)
                        for n in range(2 * STEPS + 4):
                            if n < 2 * STEPS:
                                scores(a, n)
                            if 1 <= n <= 2 * STEPS:
                                weigh_values(a, n - 1)
                            blocks, turn = max_plan(a, n)
                            for j in blocks:
                                max_block(a, j)
                            if turn is not None:
                                turn_max(a, turn)
                            if n >= 10 and n % NT == 2:
                                sum_rows(a, n // NT - 1)

                    def parts_attention():
                        pe.wait_ge(rows_in[0], 16 * (NH + MULTI))
                        for n in range(STEPS + 1):
                            if n < STEPS:
                                q, t = n // NT, n % NT
                                if n >= 2:
                                    pe.wait_ge(mexp_done, n - 1)
                                for m in range(MULTI):
                                    mm = pe.matmul(ps[:, SC + 2 * (n % 2) + m, :], km[:, m, t * P:(t + 1) * P],
                                                   qm[:, m, q * HALF:(q + 1) * HALF], start=True, stop=True)
                                mm.then_inc(ms_ready, 1)
                            if n >= 1:
                                q, t = (n - 1) // NT, (n - 1) % NT
                                if n == 1:
                                    small_turn()
                                    pe.wait_ge(o_taken[0], 4)
                                if n == NT + 1:
                                    small_turn()
                                    pe.wait_ge(mo_taken, 1)
                                pe.wait_ge(mexp_done, n)
                                for m in range(MULTI):
                                    pe.matmul(ps[MD * m:MD * (m + 1), OB, :], vm[:, t, MD * m:MD * (m + 1)],
                                              prob[:, (n - 1) % 3, m, :], start=(t == 0), stop=(t == NT - 1))
                                for m in range(MULTI):
                                    mm = pe.matmul(ps[MD * m:MD * (m + 1), GL, :], w("ones")[:, 0:MD],
                                                   prob[:, (n - 1) % 3, m, :], start=(t == 0), stop=(t == NT - 1))
                                mm.then_inc(mpv_done, 1)

                    group_stats("pre")
                    pe.wait_ge(dve_done, DV["x1"])
                    project(MX, sa1w[:, :], x1, "conv1", 96)
                    group_stats("norm")
                    pe.wait_ge(dve_done, DV["xh_a"])
                    project(SC + 2, w("wk"), xh, "k_a")
                    project(SC, w("wq"), xh, "q_a")
                    pe.wait_ge(dve_done, DV["conv_in"])
                    for h in range(2):
                        for dy in range(3):
                            mm = pe.matmul(ps[0:HD, MX + h, :], sa2w[:, dy, :],
                                           conv_in[:, 16 * h + dy:16 * h + dy + 16, :].rearrange("p y x -> p (y x)"),
                                           start=(dy == 0), stop=(dy == 2))
                    mm.then_inc(pe_done, PE.one("conv2"))
                    pe.wait_ge(dve_done, DV["conv2"])
                    for h in range(2):
                        mm = pe.matmul(ps[:, MX + h, :], sa3w[:, :], conv2[:, h * HALF:(h + 1) * HALF], start=True, stop=True)
                    mm.then_inc(pe_done, PE.one("conv3"))
                    pe.wait_ge(dve_done, DV["q_rem_a"])
                    values(SC, w("wv"), "v_a")
                    values(SC + 2, w("wvm"), "vm")
                    pe.wait_ge(dve_done, DV["v_a"])
                    pe.wait_ge(act_done, AC["vm"])
                    for m in range(MULTI):
                        for h in range(2):
                            mm = pe.matmul(ps[:, SC + 2 * m + h, :], w(f"wkm{m}"), xh[:, h * HALF:(h + 1) * HALF],
                                           start=True, stop=True)
                    mm.then_inc(pe_done, PE.one("km"))
                    pe.wait_ge(dve_done, DV["kmh"])
                    for m in range(MULTI):
                        for h in range(2):
                            mm = pe.matmul(ps[:, SC + 2 * m + h, :], w(f"wqm{m}"), gated[:, h * HALF:(h + 1) * HALF],
                                           start=True, stop=True)
                    mm.then_inc(pe_done, PE.one("qm"))
                    pe.wait_ge(dve_done, DV["qmh"])
                    attention(0)
                    parts_attention()

                    pe.wait_ge(o_scaled[0], 4)
                    pe.wait_ge(mo_scaled, 2)
                    for q in range(2):
                        pe.matmul(ps[:, SC + q, :], w("ffa0"), oatt[:, q, :], start=True, stop=False)
                        pe.matmul(ps[:, SC + q, :], w("ffa1"), oatt[:, 2 + q, :], start=False, stop=False)
                        mm = pe.matmul(ps[:, SC + q, :], w("ffb"), omul[:, q * HALF:(q + 1) * HALF], start=False, stop=True)
                    mm.then_inc(pe_done, PE.one("ff1"))
                    pe.wait_ge(dve_done, DV["ff_act"])
                    project(SC + 2, w("ff2"), tb, "ff2")
                    pe.wait_ge(act_done, AC["ff2"])
                    project(SC, w("out"), ta, "outp")
                    group_stats("post")

                    pe.wait_ge(dve_done, DV["xr"])
                    transposes(SC + 2, lambda t: x1[:, t * P:(t + 1) * P], "tr_x")
                    pe.wait_ge(dve_done, DV["ln_b"])
                    transposes(SC, lambda t: lnt[:, t, :], "tr_n_b")
                    pe.wait_ge(act_done, AC["xh_b"])
                    project(SC + 2, w("wkB"), xh, "k_b")
                    project(SC, w("wqB"), xh, "q_b")
                    pe.wait_ge(dve_done, DV["q_rem_b"])
                    values(SC, w("wvB"), "v_b")
                    pe.wait_ge(dve_done, DV["v_b"])
                    attention(1)
                    pe.wait_ge(o_scaled[1], 4)
                    for f in range(4):
                        for t in range(4):
                            mm = pe.transpose(ps[:, SC + f, t * P:(t + 1) * P], oatt[:, f, t * P:(t + 1) * P], w("ident"))
                    mm.then_inc(pe_done, PE.one("tr_o"))

                    pe.wait_ge(dve_done, DV["ln_e"])
                    transposes(SC, lambda t: lnt[:, t, :], "tr_n_e")
                    pe.wait_ge(act_done, AC["xh_e"])
                    small_turn()
                    for t in range(NT):
                        mm = pe.matmul(ps[:, GL, t * NE:(t + 1) * NE], xh[:, t * P:(t + 1) * P], gww[:, :],
                                       start=True, stop=True)
                    mm.then_inc(small_full, 1)
                    pe.wait_ge(dve_done, DV["gates"])
                    transposes(MX, lambda t: gate[:, t, :], "tr_g", NE)
                    pe.wait_ge(dve_done, DV["gate_t"])
                    for t in range(NT):
                        mm = pe.matmul(ps[:, MX + t // 4, (t % 4) * P:(t % 4 + 1) * P], gate_t[:, t * P:(t + 1) * P],
                                       b2w[:, :], start=True, stop=True)
                    mm.then_inc(pe_done, PE.one("b2"))

                    def hidden(u):
                        e, h = u // 2, u % 2
                        for c in range(NC):
                            if u:
                                pe.wait_ge(gelu_done, NC * (u - 1) + c + 1)
                            pe.matmul(ps[:, SC + c, :], w1w[:, e, c * P:(c + 1) * P], xh[:, h * HALF:(h + 1) * HALF],
                                      start=True, stop=True).then_inc(hid_ready, 1)

                    def expert_out(u):
                        e = u // 2
                        pe.wait_ge(gelu_done, NC * (u + 1))
                        if u >= 2:
                            pe.wait_ge(y_used, u - 1)
                        for t in range(4):
                            for c in range(NC):
                                mm = pe.matmul(ps[:, MX + u % 2, t * P:(t + 1) * P], hid[:, u % 2, c, t * P:(t + 1) * P],
                                               w2w[:, e, c, :], start=(c == 0), stop=(c == NC - 1))
                        mm.then_inc(y_ready, 1)

                    for u in range(2 * NE + 1):
                        if u < 2 * NE:
                            hidden(u)
                        if u == 1:
                            pe.wait_ge(dve_done, DV["b2"])
                        if u >= 1:
                            expert_out(u - 1)
                    pe.wait_ge(y_used, 2 * NE)
                    transposes(SC, lambda t: tok[:, t, :], "tr_out")

                @block.scalar
                def _(act):
                    def evacuate(dst, bank, after, name, rows=P, **kw):
                        act.wait_ge(pe_done, PE[after])
                        act.activation(dst, halves(bank, rows), kw.pop("func", ACT.Copy), **kw
                                       ).then_inc(act_done, AC.one(name))

                    def parts_of(a):
                        b = AB[a]
                        evacuate(two(parts[:, 0, 0, :]), SC + 2, f"k_{b}", f"k1_{b}")
                        evacuate(two(parts[:, 1, 0, :]), SC, f"q_{b}", f"q1_{b}")
                        for i, t in enumerate("kq"):
                            act.wait_ge(dve_done, DV[f"{t}_rem_{b}"])
                            act.activation(parts[:, i, 1, :], rem[i], ACT.Copy).then_inc(act_done, AC.one(f"{t}2_{b}"))

                    def exps(a):
                        for n in range(2 * STEPS):
                            if n >= 3:
                                act.wait_ge(pv_done[a], n - 2)
                            for pair in range(2):
                                act.wait_ge(scores_ready[a], 2 * n + pair + 1)
                                act.activation(prob[:, n % 3, 2 * pair:2 * pair + 2, :], halves(SC + 2 * pair), ACT.Exp,
                                               scale=HD ** -0.5).then_inc(exp_done[a], 1)

                    evacuate(two(ta[0:96, :]), MX, "conv1", "tanh1", 96, func=ACT.Tanh, bias=half_b[0:96, 1:2], scale=0.5)
                    parts_of(0)
                    evacuate(two(ta[0:HD, :]), MX, "conv2", "tanh2", HD, func=ACT.Tanh, bias=half_b[0:HD, 2:3], scale=0.5)
                    evacuate(two(ta[:, :]), MX, "conv3", "tanh3", func=ACT.Tanh, bias=half_b[:, 3:4], scale=0.5)
                    evacuate(vm[:, :, :].rearrange("p (a t) c -> p a (t c)", a=2), SC + 2, "vm", "vm")
                    act.wait_ge(pe_done, PE["km"])
                    act.activation(km[0:MD, :, :].rearrange("p m (a s) -> p (m a) s", a=2), ps[0:MD, SC:SC + 4, :],
                                   ACT.Copy).then_inc(act_done, AC.one("km"))
                    act.wait_ge(pe_done, PE["qm"])
                    act.activation(qm[0:MD, :, :].rearrange("p m (a s) -> p (m a) s", a=2), ps[0:MD, SC:SC + 4, :],
                                   ACT.Copy, scale=0.5).then_inc(act_done, AC.one("qm"))
                    act.wait_ge(dve_done, DV["q3_a"])
                    exps(0)
                    act.wait_ge(pv_done[0], 2 * STEPS)
                    for n in range(STEPS):
                        if n >= 3:
                            act.wait_ge(mpv_done, n - 2)
                        act.wait_ge(ms_ready, n + 1)
                        act.activation(prob[:, n % 3, 0:2, :], halves(SC + 2 * (n % 2)), ACT.Exp,
                                       scale=MD ** -0.5).then_inc(mexp_done, 1)
                    act.wait_ge(mo_scaled, 2)
                    evacuate(two(ta[:, :]), SC, "ff1", "tanh_ff", func=ACT.Tanh, bias=half_b[:, 0:1], scale=0.5)
                    act.wait_ge(dve_done, DV["ff_act"])
                    evacuate(two(ta[:, :]), SC + 2, "ff2", "ff2", func=ACT.Identity, bias=v("ff_b2"))
                    evacuate(two(tb[:, :]), SC, "outp", "outp", func=ACT.Identity, bias=v("out_b"))
                    evacuate(tok[:, :, :].rearrange("p (a t) c -> p a (t c)", a=2), SC + 2, "tr_x", "tok")
                    evacuate(two(xh[:, :]), SC, "tr_n_b", "xh_b")
                    parts_of(1)
                    act.wait_ge(dve_done, DV["q3_b"])
                    exps(1)
                    evacuate(two(xh[:, :]), SC, "tr_n_e", "xh_e")
                    act.wait_ge(dve_done, DV["gate_diff"])
                    act.activation(ex[:, :, :], logit[:, :, :], ACT.Exp).then_inc(act_done, AC.one("gate_exp"))
                    for u in range(2 * NE):
                        if u >= 2:
                            act.wait_ge(y_ready, u - 1)
                        for c in range(NC):
                            act.wait_ge(hid_ready, NC * u + c + 1)
                            act.activation(hid[:, u % 2, c, :], ps[:, SC + c, :], ACT.Gelu,
                                           bias=b1w[:, u // 2, c:c + 1]).then_inc(gelu_done, 1)
                    evacuate(two(tb[:, :]), SC, "tr_out", "result")

                @block.vector
                def _(dve):
                    chain = Turns()
                    small = Turns()
                    full = Turns()

                    def link(ins):
                        ins.then_inc(dve_chain, 1)
                        dve.wait_ge(dve_chain, chain.next())

                    def done(ins, name):
                        ins.then_inc(dve_done, DV.one(name))
                        dve.wait_ge(dve_done, DV[name])

                    def small_turn():
                        small.next()
                        dve.wait_ge(small_full, full.next())

                    def group_coefs(src, gamma, beta, eps, name):
                        for h in range(2):
                            link(dve.bn_stats(st[:, h, :], src[:, h * HALF:(h + 1) * HALF]))
                        link(dve.bn_aggr(mv[:, 0, :], st[:, 0:2, :]))
                        dve.scalar_tensor_tensor(out=mv[:, 0, 1:2], in0=mv[:, 0, 0:1], scalar=mv[:, 0, 0:1],
                                                 in1=mv[:, 0, 1:2], op0=ALU.mult, op1=ALU.add
                                                 ).then_inc(dve_done, DV.one(f"{name}_stats"))
                        small_turn()
                        dve.tensor_copy(gs[:, :], ps[:, GL, 0:2]).then_inc(small_free, 1)
                        dve.wait_ge(small_free, small.n)
                        link(dve.tensor_tensor(nb[:, 0:1], gs[:, 0:1], gs[:, 0:1], ALU.mult))
                        link(dve.scalar_tensor_tensor(out=vn[:, 0:1], in0=nb[:, 0:1], scalar=-1.0, in1=gs[:, 1:2],
                                                      op0=ALU.mult, op1=ALU.add))
                        dve.tensor_scalar(vn[:, 0:1], vn[:, 0:1], 0.0, eps, ALU.max, ALU.add
                                          ).then_inc(dve_done, DV.one(f"{name}_var"))
                        dve.wait_ge(pool_done, PL[f"{name}_rstd"])
                        link(dve.tensor_tensor(ca[:, :], rs[:, 0:1], gamma, ALU.mult))
                        link(dve.tensor_tensor(nb[:, 0:1], gs[:, 0:1], ca[:, :], ALU.mult))
                        link(dve.tensor_tensor(cb[:, :], beta, nb[:, 0:1], ALU.subtract))

                    def twice_silu(rows, bias, bank, tanh):
                        dve.wait_ge(act_done, AC[tanh])
                        return dve.tensor_scalar(two(tb[0:rows, :]), halves(bank, rows), bias, 0.5, ALU.add, ALU.mult)

                    def remainders(a):
                        b = AB[a]
                        for i, (t, bank) in enumerate((("k", SC + 2), ("q", SC))):
                            dve.wait_ge(act_done, AC[f"{t}1_{b}"])
                            dve.tensor_tensor(two(rem[i]), halves(bank), two(parts[:, i, 0, :]), ALU.subtract
                                              ).then_inc(dve_done, DV.one(f"{t}_rem_{b}"))
                        for i, t in enumerate("kq"):
                            dve.wait_ge(act_done, AC[f"{t}2_{b}"])
                            dve.tensor_tensor(parts[:, i, 2, :], rem[i], parts[:, i, 1, :], ALU.subtract
                                              ).then_inc(dve_done, DV.one(f"{t}3_{b}"))

                    def take_values(a):
                        b = AB[a]
                        dve.wait_ge(pe_done, PE[f"v_{b}"])
                        for h in range(2):
                            ins = dve.tensor_copy(va[:, 4 * h:4 * h + 4, :, 0:HD],
                                                  ps[:, SC + h, :].rearrange("p (t h d) -> p t h d", t=4, h=NH))
                            if h == 0:
                                ins.then_inc(dve_chain, 1)
                                chain.next()
                        ins.then_inc(dve_done, DV.one(f"v_{b}"))

                    def reduce_block(a, j):
                        u, t, k = max_blocks(a)[j]
                        dve.wait_ge(blocks_ready[a], j + 1)
                        dve.tensor_reduce(blockmax[:, u, t, k:k + 1], ps[:, MX + j % 2, :], AX.X, ALU.max
                                          ).then_inc(blocks_used[a], 1)
                        if j % 16 == 15:
                            dve.wait_ge(blocks_used[a], j + 1)
                            dve.tensor_reduce(negmax[:, u, :], blockmax[:, u, :, :], AX.X, ALU.max, negate=True
                                              ).then_inc(max_ready[a], 1)

                    def split_max(a, u):
                        small_turn()
                        src = ps[0:NT, GL, 0:P]
                        if u >= NH:
                            dve.tensor_copy(maxrow_m[:, u - NH, :], src).then_inc(rows_split[a], 1)
                            dve.wait_ge(rows_split[a], u + 1)
                            dve.tensor_copy(esum[0:NT, :], maxrow_m[:, u - NH, 0:NT]).then_inc(small_free, 1)
                            return
                        link(dve.tensor_copy(maxrow[:, u, 0, :], src))
                        dve.tensor_tensor(rowrem, src, maxrow[:, u, 0, :], ALU.subtract).then_inc(small_free, 1)
                        dve.wait_ge(small_free, small.n)
                        link(dve.tensor_copy(maxrow[:, u, 1, :], rowrem))
                        dve.tensor_tensor(maxrow[:, u, 2, :], rowrem, maxrow[:, u, 1, :], ALU.subtract
                                          ).then_inc(rows_split[a], 1)
                        dve.wait_ge(rows_split[a], u + 1)

                    rowrem = gate_t[:, 0:P]

                    def take_output(a, f):
                        dve.wait_ge(pv_done[a], NT * (f + 1))
                        dve.tensor_copy(oatt[:, f, :], ps[:, OB, :]).then_inc(o_taken[a], 1)

                    def scale_output(a, f):
                        small_turn()
                        dve.reciprocal(rec[:, :], ps[:, GL, :]).then_inc(small_free, 1)
                        dve.wait_ge(small_free, small.n)
                        dve.tensor_tensor(oatt[:, f, :], oatt[:, f, :], rec[:, :], ALU.mult).then_inc(o_scaled[a], 1)
                        dve.wait_ge(o_scaled[a], f + 1)

                    def attention(a):
                        for j in range(64):
                            reduce_block(a, j)
                            if j % 16 == 12 and j > 16:
                                split_max(a, j // 16 - 1)
                        split_max(a, 3)
                        for n in range(2 * STEPS + 4):
                            if n and n % NT == 0 and n <= 2 * STEPS:
                                take_output(a, n // NT - 1)
                            blocks, turn = max_plan(a, n)
                            for j in blocks:
                                reduce_block(a, j)
                            if turn is not None:
                                split_max(a, turn)
                            if n >= 11 and n % NT == 3:
                                scale_output(a, n // NT - 1)

                    def layer_norm(name):
                        for t in range(NT):
                            ins = dve.bn_stats(st[:, t, :], tok[:, t, :])
                            ins.then_inc(dve_chain, 1)
                            chain.next()
                        dve.wait_ge(dve_chain, chain.n)
                        for t in range(NT):
                            dve.bn_aggr(mv[:, t, :], st[:, t, :]).then_inc(dve_chain, 1)
                            chain.next()
                        dve.wait_ge(dve_chain, chain.n)
                        dve.tensor_scalar(vn[:, :], mv[:, :, 1], 0.0, 1e-5, ALU.max, ALU.add
                                          ).then_inc(dve_done, DV.one(f"ln_var_{name}"))
                        dve.wait_ge(pool_done, PL[f"ln_rstd_{name}"])
                        link(dve.scalar_tensor_tensor(out=nb[:, :], in0=mv[:, :, 0], scalar=-1.0, in1=rs[:, :],
                                                      op0=ALU.mult, op1=ALU.mult))
                        for t in range(NT):
                            ins = dve.tensor_scalar(lnt[:, t, :], tok[:, t, :], rs[:, t:t + 1], nb[:, t:t + 1],
                                                    ALU.mult, ALU.add)
                            if t < NT - 1:
                                ins.then_inc(dve_chain, 1)
                                chain.next()
                        ins.then_inc(dve_done, DV.one(f"ln_{name}"))

                    dve.wait_ge(x_in, 16)
                    group_coefs(xin, v("pre_g"), v("pre_b"), 1e-6, "pre")
                    link(dve.scalar_tensor_tensor(out=x1[:, :], in0=xin[:, :], scalar=ca[:, :], in1=posw[:, :],
                                                  op0=ALU.mult, op1=ALU.add))
                    done(dve.tensor_scalar(x1[:, :], x1[:, :], cb[:, :], None, ALU.add), "x1")
                    group_coefs(x1, v("norm_g"), v("norm_b"), 1e-6, "norm")
                    done(dve.tensor_scalar(xh[:, :], x1[:, :], ca[:, :], cb[:, :], ALU.mult, ALU.add), "xh_a")
                    done(twice_silu(96, v("sa_b1", 96), MX, "tanh1"), "u1")
                    for dx in range(3):
                        q = slice(32 * dx, 32 * dx + 32)
                        lo, hi = max(0, 1 - dx), min(SIDE, SIDE + 1 - dx)
                        ins = dve.scalar_tensor_tensor(
                            out=conv_in[q, 1:SIDE + 1, lo:hi],
                            in0=ta[q, :].rearrange("p (y x) -> p y x", x=SIDE)[:, :, lo + dx - 1:hi + dx - 1],
                            scalar=1.0,
                            in1=tb[q, :].rearrange("p (y x) -> p y x", x=SIDE)[:, :, lo + dx - 1:hi + dx - 1],
                            op0=ALU.add, op1=ALU.mult)
                        if dx < 2:
                            ins.then_inc(dve_chain, 1)
                            chain.next()
                    done(ins, "conv_in")
                    remainders(0)
                    done(twice_silu(HD, v("sa_b2", HD), MX, "tanh2"), "u2")
                    dve.scalar_tensor_tensor(out=conv2[:, :], in0=ta[0:HD, :], scalar=1.0, in1=tb[0:HD, :],
                                             op0=ALU.add, op1=ALU.mult).then_inc(dve_done, DV.one("conv2"))
                    take_values(0)
                    dve.wait_ge(act_done, AC["tanh3"])
                    dve.scalar_tensor_tensor(out=gated[:, :], in0=ta[:, :], scalar=1.0, in1=x1[:, :],
                                             op0=ALU.add, op1=ALU.mult).then_inc(dve_done, DV.one("gated"))
                    dve.wait_ge(act_done, AC["km"])
                    dve.tensor_copy(kmh[:, :, :].rearrange("p m (a s) -> p (m a) s", a=2), ps[:, SC:SC + 4, :]
                                    ).then_inc(dve_done, DV.one("kmh"))
                    dve.wait_ge(act_done, AC["qm"])
                    qmh_v = qmh[:, :, :].rearrange("p m (a s) -> p (m a) s", a=2)
                    link(dve.tensor_scalar(qmh_v, ps[:, SC:SC + 4, :], 0.5, None, ALU.mult))
                    for b in range(2):
                        ins = dve.scalar_tensor_tensor(
                            out=qmh[MD:P, b, :], in0=ps[MD:P, SC + 2 * b:SC + 2 * b + 2, :].rearrange("p a s -> p (a s)"),
                            scalar=0.5, in1=qmh[MD:P, b, :], op0=ALU.mult, op1=ALU.subtract)
                        if b == 0:
                            ins.then_inc(dve_chain, 1)
                            chain.next()
                    ins.then_inc(dve_done, DV.one("qmh"))
                    attention(0)
                    for q in range(2):
                        dve.wait_ge(mpv_done, NT * (q + 1))
                        dve.tensor_copy(tb[:, 0:HALF], ps[:, OB, :]).then_inc(mo_taken, 1)
                        dve.wait_ge(mo_taken, q + 1)
                        small.next()
                        dve.reciprocal(rec[:, :], ps[:, GL, :]).then_inc(small_free, 1)
                        dve.wait_ge(small_free, small.n)
                        dve.tensor_tensor(omul[:, q * HALF:(q + 1) * HALF], tb[:, 0:HALF], rec[:, :], ALU.mult
                                          ).then_inc(mo_scaled, 1)
                        dve.wait_ge(mo_scaled, q + 1)

                    link(twice_silu(P, v("ff_b1"), SC, "tanh_ff"))
                    dve.scalar_tensor_tensor(out=tb[:, :], in0=ta[:, :], scalar=1.0, in1=tb[:, :],
                                             op0=ALU.add, op1=ALU.mult).then_inc(dve_done, DV.one("ff_act"))
                    dve.wait_ge(act_done, AC["outp"])
                    group_coefs(tb, v("post_g"), v("post_b"), 1e-6, "post")
                    link(dve.scalar_tensor_tensor(out=x1[:, :], in0=tb[:, :], scalar=ca[:, :], in1=xin[:, :],
                                                  op0=ALU.mult, op1=ALU.add))
                    dve.tensor_scalar(x1[:, :], x1[:, :], cb[:, :], None, ALU.add).then_inc(dve_done, DV.one("xr"))

                    dve.wait_ge(act_done, AC["tok"])
                    layer_norm("b")
                    remainders(1)
                    take_values(1)
                    attention(1)
                    dve.wait_ge(pe_done, PE["tr_o"])
                    for f in range(4):
                        g, q = f // 2, f % 2
                        t = tok[:, 4 * q:4 * q + 4, 64 * g:64 * g + 64].rearrange("p t (j d) -> p t j d", d=HD)
                        o = ps[:, SC + f, :].rearrange("p (t j r) -> p t j r", t=4, r=2 * HD)[:, :, :, 0:HD]
                        ins = dve.tensor_tensor(t, t, o, ALU.add)
                        if f < 3:
                            ins.then_inc(dve_chain, 1)
                            chain.next()
                    done(ins, "tok2")
                    dve.wait_ge(dve_chain, chain.n)
                    layer_norm("e")

                    small_turn()
                    dve.tensor_tensor(logit[:, :, :], ps[:, GL, 0:NT * NE].rearrange("p (t e) -> p t e", t=NT),
                                      gbw[:, :, :], ALU.add).then_inc(small_free, 1)
                    dve.wait_ge(small_free, small.n)
                    for t in range(NT):
                        link(dve.max(top[:, t, :], logit[:, t, :]))
                    for t in range(NT):
                        link(dve.max_index(topi[:, t, :], top[:, t, :], logit[:, t, :]))
                    link(dve.tensor_copy(topf[:, :, :], topi[:, :, 0:2]))
                    done(dve.tensor_tensor(logit[:, :, :], logit[:, :, :], top[:, :, 0:1].to_broadcast([P, NT, NE]),
                                           ALU.subtract), "gate_diff")
                    link(dve.tensor_tensor(oh[:, :, :], iow[:, :, :], topf[:, :, 0:1].to_broadcast([P, NT, NE]),
                                           ALU.is_equal))
                    link(dve.tensor_tensor(gate[:, :, :], iow[:, :, :], topf[:, :, 1:2].to_broadcast([P, NT, NE]),
                                           ALU.is_equal))
                    link(dve.tensor_tensor(gate[:, :, :], gate[:, :, :], oh[:, :, :], ALU.add))
                    dve.wait_ge(act_done, AC["gate_exp"])
                    link(dve.tensor_reduce(esum[:, :], ex[:, :, :], AX.X, ALU.add))
                    link(dve.reciprocal(erec[:, :], esum[:, :]))
                    link(dve.tensor_tensor(gate[:, :, :], gate[:, :, :], ex[:, :, :], ALU.mult))
                    done(dve.tensor_tensor(gate[:, :, :], gate[:, :, :],
                                           erec[:, :].unsqueeze(2).to_broadcast([P, NT, NE]), ALU.mult), "gates")
                    dve.wait_ge(pe_done, PE["tr_g"])
                    dve.tensor_copy(two(gate_t[:, :]), halves(MX, NE)).then_inc(dve_done, DV.one("gate_t"))
                    dve.wait_ge(pe_done, PE["b2"])
                    tv = tok[:, :, :].rearrange("p (a t) c -> p a (t c)", a=2)
                    done(dve.tensor_tensor(tv, tv, halves(MX), ALU.add), "b2")
                    for u in range(2 * NE):
                        e, h = u // 2, u % 2
                        dve.wait_ge(y_ready, u + 1)
                        if h == 0 and u:
                            dve.wait_ge(y_used, u)
                            dve.wait_ge(dve_chain, chain.n)
                        for t in range(4):
                            tt = 4 * h + t
                            ins = dve.scalar_tensor_tensor(out=tok[:, tt, :], in0=ps[:, MX + u % 2, t * P:(t + 1) * P],
                                                           scalar=gate[:, tt, e:e + 1], in1=tok[:, tt, :],
                                                           op0=ALU.mult, op1=ALU.add)
                            if t < 3:
                                ins.then_inc(dve_chain, 1)
                                chain.next()
                        ins.then_inc(y_used, 1)

            nc.all_engine_barrier(sems_to_clear=cleared)


def kernel(**inputs):
    import numpy as np
    import concourse.bacc as bacc
    from concourse.bass_utils import run_bass_kernel_spmd

    g = {k: np.asarray(v) for k, v in inputs.items()}
    L0 = {k[len("L0_conv_"):]: v for k, v in g.items() if k.startswith("L0_conv_")}
    NB = g["x"].shape[0]
    f32 = np.float32

    eye = np.eye(P, dtype=f32)
    group = np.kron(np.eye(P // 4), np.full((4, 4), 0.25)).astype(f32)
    spread_sum = np.zeros((P, P), f32)
    for j in range(4):
        spread_sum[32 * j + HD, 32 * j:32 * j + 32] = 1.0

    def strips(wt, grp):
        o = np.zeros((P, P), f32)
        for j in range(4):
            o[32 * j:32 * j + HD] = wt[64 * grp + HD * j:64 * grp + HD * (j + 1)]
        return o

    ff1 = L0["ff_w1"].T
    qkv = g["L1_attn_w_qkv"]
    table = {
        "wk": L0["wk"].T, "wq": L0["wq"].T, "wv": L0["wv"].T,
        "wqB": qkv[:, 0:P], "wkB": qkv[:, P:2 * P], "wvB": qkv[:, 2 * P:],
        "ffa0": strips(ff1[:P], 0), "ffa1": strips(ff1[:P], 1), "ffb": ff1[P:],
        "ff2": L0["ff_w2"].T, "out": L0["out_w"].T,
        "wvm": np.concatenate([L0["wv0"].T, L0["wv1"].T], 1),
        "wkm0": np.concatenate([L0["wk0"].T] * 2, 1), "wkm1": np.concatenate([L0["wk1"].T] * 2, 1),
        "wqm0": np.concatenate([L0["wq0"].T] * 2, 1), "wqm1": np.concatenate([L0["wq1"].T] * 2, 1),
        "ident": eye, "group": group, "spread_sum": spread_sum, "ones": np.ones((P, P), f32),
    }

    def column(vals, at=(0,)):
        o = np.zeros(P, f32)
        for a in at:
            o[a:a + len(vals)] = vals
        return o

    vtable = {n: L0[n] for n in VECTORS if n in L0}
    vtable["sa_b1"] = column(L0["sa_b1"], (0, 32, 64))
    vtable["sa_b2"] = column(L0["sa_b2"])
    vtable["sa_b3"] = np.broadcast_to(L0["sa_b3"], (P,))
    vtable["neg_half"] = np.full(P, -0.5, f32)
    s1 = L0["sa_w1"].reshape(HD, P).T
    sa1 = np.zeros((P, 96), f32)
    sa2 = np.zeros((96, 3, HD), f32)
    for dx in range(3):
        sa1[:, 32 * dx:32 * dx + HD] = s1
        sa2[32 * dx:32 * dx + HD] = L0["sa_w2"][:, :, :, dx].transpose(1, 2, 0)
    arrays = {
        "x": g["x"].reshape(NB, P, S),
        "pos": L0["pos_emb"].reshape(P, S),
        "wts": np.stack([table[n] for n in WEIGHTS], 1),
        "vecs": np.stack([vtable[n] for n in VECTORS], 1),
        "sa1": sa1, "sa2": sa2,
        "sa3": np.repeat(L0["sa_w3"].reshape(HD, 1), P, 1),
        "w1": g["L1_ffn_w1"].transpose(1, 0, 2),
        "b1": g["L1_ffn_b1"].reshape(NE, NC, P).transpose(2, 0, 1),
        "w2": g["L1_ffn_w2"].reshape(NE, NC, P, P).transpose(2, 0, 1, 3),
        "b2": g["L1_ffn_b2"],
        "gw": g["L1_ffn_gate_w"],
        "gb": np.broadcast_to(g["L1_ffn_gate_b"], (P, NT, NE)),
        "iota": np.broadcast_to(np.arange(NE, dtype=f32), (P, NT, NE)),
    }
    nc = bacc.Bacc("TRN2", target_bir_lowering=False, num_devices=1)
    feed, args = {}, []
    for name, a in arrays.items():
        a = np.ascontiguousarray(a)
        feed[f"in_{name}"] = a
        args.append(nc.dram_tensor(f"in_{name}", a.shape, mybir.dt.from_np(a.dtype), kind="ExternalInput").ap())
    out = nc.dram_tensor("out_0", (NB, P, S), F32, kind="ExternalOutput").ap()
    build(nc, *args, out)
    r = run_bass_kernel_spmd(nc, [feed], core_ids=[0])
    return r.results[0]["out_0"].reshape(NB, P, SIDE, SIDE)
```

```python
from contextlib import ExitStack

import concourse.bass as bass
from concourse import mybir

F32 = mybir.dt.float32
BF16 = mybir.dt.bfloat16
U32 = mybir.dt.uint32
ACT = mybir.ActivationFunctionType
ALU = mybir.AluOpType
AX = mybir.AxisListType

P = 128
S = 1024
HALF = 512
NT = S // P
NH = 8
HD = P // NH
GH = 4
K_PARTS = (0, 1, 0, 1, 2, 0)
Q_PARTS = (0, 0, 1, 1, 0, 2)
PIECES = len(K_PARTS)
ROWS = PIECES * HD
NE = 8
HID = 512
NC = HID // P
SIDE = 32
MULTI = 2
MD = 64
STEPS = 16
UNITS = 2 * NE
EPS_GN, EPS_LN = 1e-6, 1e-5

SC = 0
OB = 4
MX = 5
SM = 7

WEIGHTS = ["wk", "wq", "wv", "wkB", "wqB", "wvB", "ffa0", "ffa1", "ffb", "ff2", "out",
           "wvm", "wkm0", "wkm1", "wqm0", "wqm1", "ident", "group", "spread_sum", "ones"]
VECTORS = ["pre_g", "pre_b", "norm_g", "norm_b", "post_g", "post_b", "ff_b1", "ff_b2", "out_b",
           "sa_b1", "sa_b2", "sa_b3", "neg_half"]

FAMILIES = {"a0": (0, 0, 0), "a1": (0, 64, 4), "b": (1, 0, 0)}

CONV_WINDOW = {0: ["tro0"], 1: ["tro1"], 2: ["tro2"], 3: ["tro3"], 4: ["turn_a1_4"], 5: ["km00"], 6: ["trn0"],
               7: ["turn_a1_5"], 8: ["trn1"], 9: ["logits"], 10: ["turn_a1_6", "sum0"], 11: ["km01"], 12: ["km10"],
               13: ["turn_a1_7"], 14: ["trg0"], 15: ["trg1"], 16: ["b20"], 17: ["b21"], 18: ["sum1"], 19: ["km11"],
               20: ["qm00"], 21: ["qm01"], 22: ["qm10"], 23: ["qm11"], 26: ["sum2"], 27: ["turn_a1_8"],
               30: ["turn_a1_9"]}
PARTS_WINDOW = {2: ["sum3"]}
EXPERT_WINDOW = {2: ["ff1"], 4: ["ff2"], 5: ["outp"], 7: ["post"], 9: ["tr_x"], 12: ["tr_nb"], 13: ["kB"],
                 15: ["qB"], 17: ["vB"], 23: ["turn_b_0"], 26: ["turn_b_1"], 28: ["turn_b_2"], 31: ["turn_b_3"]}
TOKEN_WINDOW = {1: ["pre"], 4: ["turn_b_4"], 5: ["norm"], 7: ["turn_b_5"], 8: ["kA0"], 9: ["kA1"], 10: ["turn_b_6"],
                11: ["qA0"], 12: ["qA1"], 13: ["turn_b_7"], 14: ["vA0"], 15: ["vA1"], 16: ["c10"], 17: ["c11"],
                19: ["c20"], 20: ["c21"], 21: ["c30"], 22: ["turn_a0_0"], 23: ["c31"], 24: ["vm0"],
                25: ["turn_a0_1"], 26: ["vm1"], 28: ["turn_a0_2"], 31: ["turn_a0_3"]}
LAST_NORM = ("tro", "trn", "logits", "trg", "b2")


def conv_blocks(n):
    if n < 13:
        return range(64 + 5 * n, min(64 + 5 * n + 5, 128))
    return range(128 + 5 * (n - 22), min(128 + 5 * (n - 22) + 5, 160)) if n >= 22 else range(0)


def expert_blocks(s):
    return range(6 * (s - 20), min(6 * (s - 20) + 6, 64)) if s >= 20 else range(0)


def token_blocks(n):
    return range(64 + 5 * n, min(64 + 5 * n + 5, 128)) if n < 13 else range(0)


def front_blocks(n):
    return range(5 * (n - 18), min(5 * (n - 18) + 5, 64)) if n >= 18 else range(0)


def block_of(j):
    return j // 16, j // 2 % NT, j % 2


def slot_of(a, g):
    return ((2, 0), (0, 1))[a][g]


def only(table, keep):
    return {n: kept for n, names in table.items() if (kept := [x for x in names if keep(x)])}


def for_front(name):
    return not name.startswith("turn_b")


def for_last_norm(name):
    return name.startswith(LAST_NORM)


class Small:

    def __init__(self, *windows):
        self.order = [x for w in windows for n in sorted(w) for x in w[n]]

    def __getitem__(self, name):
        return self.order.index(name) + 1


def build(nc, x, pos, wts, vecs, sa1, sa2, sa3, w1, b1, w2, b2, gw, gb, iota, out):
    NB = x.shape[0]
    ctx = ExitStack()
    with ctx:
        def sb(name, shape, dt=F32):
            return ctx.enter_context(nc.sbuf_tensor(name, shape, dt))

        def sem(name):
            return ctx.enter_context(nc.semaphore(name))

        ps = ctx.enter_context(nc.psum_tensor("ps", [P, 8, HALF], F32))

        wt = sb("wt", [P, len(WEIGHTS), P])
        vec = sb("vec", [P, len(VECTORS)])
        half_b = sb("half_b", [P, 4])
        posw = sb("posw", [P, S])
        sa1w = sb("sa1w", [P, 96])
        sa2w = sb("sa2w", [96, 3, HD])
        sa3w = sb("sa3w", [HD, P])
        b1w = sb("b1w", [P, NE, NC])
        b2w = sb("b2w", [NE, P])
        gww = sb("gww", [P, NE])
        gbw = sb("gbw", [P, NT, NE])
        iow = sb("iow", [P, NT, NE])

        def w(name):
            return wt[:, WEIGHTS.index(name), :]

        def v(name, n=P):
            i = VECTORS.index(name)
            return vec[0:n, i:i + 1]

        xin = sb("xin", [P, S])
        x1 = sb("x1", [P, S])
        xh = sb("xh", [P, S])
        xe = sb("xe", [P, S])
        gated = sb("gated", [P, S])
        omul = gated
        ta = sb("ta", [P, S])
        tb = sb("tb", [P, S])
        conv_in = sb("conv_in", [96, SIDE + 2, SIDE])
        low = sb("low", [HD, S])
        conv2, gate_t = low, low[0:NE, :]
        parts = sb("parts", [P, 2, 3, S], BF16)
        rem = ta
        ks = sb("ks", [ROWS + 3, 3, GH, S], BF16)
        qs = sb("qs", [ROWS + 3, 3, GH, S], BF16)
        va = [sb("va_a", [P, NT, NH, 2 * HD]),
              sb("va_b", [P, NT, NH, 2 * HD])]
        vm = sb("vm", [P, NT, P])
        km = sb("km", [MD + 1, MULTI, S])
        qm = sb("qm", [MD + 1, MULTI, S])
        shared = [sb("shared0", [P, 2, HALF]), sb("shared1", [P, 2, HALF])]
        kmh, qmh = (t[:, :, :].bitcast(BF16) for t in shared)
        w1e = [t[:, 0, :] for t in shared]
        w2e = [t[:, 1, :] for t in shared]
        prob = sb("prob", [P, 3, 4, HALF])
        oatt = sb("oatt", [P, 4, HALF])
        rec = tb[:, HALF:S]
        tok = sb("tok", [P, NT, P])
        toke = sb("toke", [P, NT, P])
        blockmax = sb("blockmax", [P, 10, NT, 2])
        negmax = sb("negmax", [P, 10, NT])
        maxrow = sb("maxrow", [NT, 2, 3, P], BF16)
        maxrow_m = sb("maxrow_m", [NT, MULTI, P])
        rowrem = sb("rowrem", [NT, P])
        st = sb("st", [P, NT, 6])
        mv = sb("mv", [P, NT, 2])
        gs = sb("gs", [P, 2])
        vn = sb("vn", [P, NT])
        rs = sb("rs", [P, NT])
        nb = sb("nb", [P, NT])
        ca = sb("ca", [P, 1])
        cb = sb("cb", [P, 1])
        orec = sb("orec", [P, 4, GH])
        logit = sb("logit", [P, NT, NE])
        top = sb("top", [P, NT, 8])
        topi = sb("topi", [P, NT, 8], U32)
        topf = sb("topf", [P, NT, 2])
        ex = sb("ex", [P, NT, NE])
        oh = sb("oh", [P, NT, NE])
        gate = sb("gate", [P, NT, NE])
        esum = sb("esum", [P, NT])
        erec = sb("erec", [P, NT])
        lnt = ta[:, :].rearrange("p (t c) -> p t c", t=NT)

        parts_dram = nc.dram_tensor("parts_dram", (2, 2, P, 3, S), BF16, kind="Internal").ap()
        maxrow_dram = nc.dram_tensor("maxrow_dram", (2, NH, NT, 3, P), BF16, kind="Internal").ap()
        maxrow_m_dram = nc.dram_tensor("maxrow_m_dram", (MULTI, NT, P), F32, kind="Internal").ap()

        weights_in, consts_set = sem("weights_in"), sem("consts_set")

        x_in = sem("x_in")
        small_full, small_free = sem("small_full"), sem("small_free")
        dve_chain = sem("dve_chain")
        parts_out = [[sem("k_out_a"), sem("q_out_a")], [sem("k_out_b"), sem("q_out_b")]]
        spread = [[sem("spread_a0"), sem("spread_a1")], [sem("spread_b0"), sem("spread_b1")]]
        blocks_ready, blocks_used, max_ready, rows_split, rows_out, rows_in = (
            {f: sem(f"{n}_{f}") for f in FAMILIES}
            for n in ("blocks_ready", "blocks_used", "max_ready", "rows_split", "rows_out", "rows_in"))
        scores_ready, exp_done, pv_done, o_taken, o_scaled = (
            [sem(f"{n}_a"), sem(f"{n}_b")] for n in ("scores_ready", "exp_done", "pv_done", "o_taken", "o_scaled"))
        ms_ready, mexp_done, mpv_done, mo_taken, mo_scaled = (
            sem("ms_ready"), sem("mexp_done"), sem("mpv_done"), sem("mo_taken"), sem("mo_scaled"))
        weights_ready, hid_ready, gelu_done = sem("weights_ready"), sem("hid_ready"), sem("gelu_done")
        y_ready, y_used, result_ready, result = sem("y_ready"), sem("y_used"), sem("result_ready"), sem("result")
        done = {name: sem(name) for name in (
            "pre_stats", "pre_var", "pre_rstd", "x1", "norm_stats", "norm_var", "norm_rstd", "xh_a",
            "k1_a", "k_rem_a", "k2_a", "k3_a", "q1_a", "q_rem_a", "q2_a", "q3_a", "v_a",
            "tanh1", "conv_in", "tanh2", "conv2", "tanh3", "gated", "vm",
            "km", "kmh", "qm", "qmh", "tanh_ff", "ff_act", "ff2", "outp", "post_stats", "post_var", "post_rstd",
            "xr", "tok", "ln_var_b", "ln_rstd_b", "ln_b", "xh_b",
            "k1_b", "k_rem_b", "k2_b", "k3_b", "q1_b", "q_rem_b", "q2_b", "q3_b", "v_b",
            "ln_var_e", "ln_rstd_e", "ln_e", "xe", "gate_diff", "gate_exp", "gates", "gate_t", "b2")}
        out_done = sem("out_done")
        cleared = range(x_in.num, out_done.num + 1)

        def cols(h):
            return slice(h * HALF, (h + 1) * HALF)

        def two(ap):
            return ap.rearrange("p (a s) -> p a s", a=2)

        def pair(rows=P):
            return ps[0:rows, OB:SM + 1:SM - OB, :]

        def pair_bank(h):
            return (OB, SM)[h]

        with nc.Block() as block:
            @block.sync
            def _(sp):
                loads = ((wt[:, :, :], wts), (vec[:, :], vecs), (posw[:, :], pos), (sa1w[:, :], sa1),
                         (sa2w[:, :, :], sa2), (sa3w[:, :], sa3), (b1w[:, :, :], b1), (b2w[:, :], b2),
                         (gww[:, :], gw), (gbw[:, :, :], gb), (iow[:, :, :], iota))
                for dst, src in loads:
                    sp.dma_start(dst, src).then_inc(weights_in, 16)
                sp.wait_ge(weights_in, 16 * len(loads))

            @block.gpsimd
            def _(pool):
                pool.memset(oatt[:, :, :], 1.0).then_inc(consts_set, 1)
                pool.memset(tok[:, :, :], 0.0).then_inc(consts_set, 1)

            @block.vector
            def _(dve):
                dve.memset(conv_in[:, :, :], 0.0).then_inc(consts_set, 1)
                dve.memset(ks[ROWS:ROWS + 3, :, :, :], 1.0).then_inc(consts_set, 1)
                for a in range(2):
                    dve.memset(va[a][:, :, :, :], 1.0).then_inc(consts_set, 1)
                dve.memset(km[MD:MD + 1, :, :], 1.0).then_inc(consts_set, 1)
                dve.wait_ge(weights_in, 16 * 11)
                for i, name in enumerate(("ff_b1", "sa_b1", "sa_b2", "sa_b3")):
                    dve.tensor_scalar(half_b[:, i:i + 1], v(name), 0.5, None, ALU.mult).then_inc(consts_set, 1)
                dve.wait_ge(consts_set, 11)

        def sync_program(sp, img, conv, experts, token, front, small):
            def spread_parts(a, i):
                sp.wait_ge(done[f"{'kq'[i]}3_{'ab'[a]}"], 2 if a == 0 else 1)
                sp.dma_start(parts_dram[a, i], parts[:, i, :, :]).then_inc(parts_out[a][i], 16)

            def spread_group(a, i, g):
                sp.wait_ge(parts_out[a][i], 16)
                for j, part in enumerate((K_PARTS, Q_PARTS)[i]):
                    dst = (ks, qs)[i][HD * j:HD * (j + 1), slot_of(a, g), :, :]
                    src = parts_dram[a, i, GH * HD * g:GH * HD * (g + 1), part, :]
                    sp.dma_start(dst, src.rearrange("(h d) s -> d h s", d=HD)).then_inc(spread[a][g], 16)

            def spread_max(f, u):
                a, _, first = FAMILIES[f]
                n = u - first + 1
                sp.wait_ge(rows_split[f], n)
                if u < NH:
                    sp.dma_start(maxrow_dram[a, u], maxrow[:, u % 2, :, :]).then_inc(rows_out[f], 16)
                    sp.wait_ge(rows_out[f], 16 * n)
                    sp.dma_start(qs[ROWS:ROWS + 3, slot_of(a, u // GH), u % GH, :].rearrange("r (t s) -> r t s", t=NT),
                                 maxrow_dram[a, u].rearrange("t r s -> r t s")).then_inc(rows_in[f], 16)
                else:
                    m = u - NH
                    sp.dma_start(maxrow_m_dram[m], maxrow_m[:, m, :]).then_inc(rows_out[f], 16)
                    sp.wait_ge(rows_out[f], 16 * n)
                    sp.dma_start(qm[MD:MD + 1, m, :],
                                 maxrow_m_dram[m:m + 1].rearrange("m t s -> m (t s)")).then_inc(rows_in[f], 16)

            def fetch(e):
                if e == 0 and conv:
                    sp.wait_ge(blocks_used["a1"], 96)
                if e >= 2:
                    sp.wait_ge(y_ready, 2 * (e - 1))
                if e >= 1:
                    sp.wait_ge(weights_ready, 32 * e)
                sp.dma_start(w1e[e % 2], w1[:, e, :]).then_inc(weights_ready, 16)
                sp.dma_start(w2e[e % 2], w2[:, e, :]).then_inc(weights_ready, 16)

            if conv:
                for u in range(4, NH + MULTI):
                    spread_max("a1", u)
            if experts:
                for e in range(5):
                    fetch(e)
            if token:
                sp.wait_ge(pv_done[0], 2 * STEPS)
                spread_parts(1, 0)
                spread_group(1, 0, 0)
                fetch(5)
                spread_parts(1, 1)
                spread_group(1, 1, 0)
                fetch(6)
                for i in range(2):
                    spread_group(1, i, 1)
                spread_max("b", 0)
                fetch(7)
                for u in range(1, 4):
                    spread_max("b", u)
            elif experts:
                for e in range(5, NE):
                    fetch(e)
            if experts:
                sp.wait_ge(result, 2)
                last = (img - 1 + NB) % NB if token else NB - 1
                sp.dma_start(out[bass.ds(last, 1)].rearrange("a p s -> (a p) s"), xe[:, :]).then_inc(out_done, 16)
            if front:
                if token:
                    sp.wait_ge(done["xr"], 1)
                nxt = (img + 1) % NB if token else 0
                sp.dma_start(xin[:, :], x[bass.ds(nxt, 1)].rearrange("a p s -> (a p) s")).then_inc(x_in, 16)
                if token:
                    for u in range(4, 7):
                        spread_max("b", u)
                spread_parts(0, 0)
                if token:
                    spread_max("b", 7)
                spread_parts(0, 1)
                for i in range(2):
                    spread_group(0, i, 0)
                if token:
                    sp.wait_ge(pv_done[1], STEPS)
                for i in range(2):
                    spread_group(0, i, 1)
                for u in range(4):
                    spread_max("a0", u)
                sp.wait_ge(spread[0][0], 16 * 2 * PIECES)
                sp.wait_ge(spread[0][1], 16 * 2 * PIECES)
                sp.wait_ge(rows_in["a0"], 16 * 4)
            if experts:
                sp.wait_ge(out_done, 16)

        def pool_program(pool, conv, experts, token, front, small):
            def rstd(name, n):
                pool.wait_ge(done[name.replace("rstd", "var")], 1)
                pool.tensor_tensor(rs[:, 0:n], vn[:, 0:n], v("neg_half").to_broadcast([P, n]),
                                   ALU.pow).then_inc(done[name], 1)

            if experts:
                rstd("ln_rstd_e", NT)
            if token:
                rstd("post_rstd", 1)
                rstd("ln_rstd_b", NT)
            if front:
                rstd("pre_rstd", 1)
                rstd("norm_rstd", 1)

        def tensor_program(pe, conv, experts, token, front, small):
            def start_small(name):
                if small[name] > 1:
                    pe.wait_ge(small_free, small[name] - 1)

            def max_block(f, j):
                a, first, _ = FAMILIES[f]
                u, t, k = block_of(j)
                n = j - first
                if n == 0:
                    if f == "a0":
                        pe.wait_ge(spread[0][0], 16 * 2 * PIECES)
                        if token:
                            pe.wait_ge(blocks_used["b"], 128)
                    if f == "b":
                        pe.wait_ge(spread[1][0], 16 * 2 * PIECES)
                        pe.wait_ge(blocks_used["a1"], 96)
                if f == "b" and j == 64:
                    pe.wait_ge(spread[1][1], 16 * 2 * PIECES)
                if u >= NH and (t, k) == (0, 0):
                    pe.wait_ge(done["kmh"], 2 * (u - NH + 1))
                    pe.wait_ge(done["qmh"], 2 * (u - NH + 1))
                if n >= 2:
                    pe.wait_ge(blocks_used[f], n - 1)
                if u < NH:
                    slot = slot_of(a, u // GH)
                    lhs, rhs = qs[0:ROWS, slot, u % GH, t * P:(t + 1) * P], ks[0:ROWS, slot, u % GH, cols(k)]
                else:
                    lhs, rhs = qmh[:, u - NH, t * P:(t + 1) * P], kmh[:, u - NH, cols(k)]
                pe.matmul(ps[:, MX + n % 2, :], lhs, rhs, start=True, stop=True).then_inc(blocks_ready[f], 1)

            def transposes(bank, src, count=4, rows=P):
                for t in range(count):
                    mm = pe.transpose(ps[0:rows, bank, t * P:(t + 1) * P], src(t), w("ident"))
                return mm

            def half_product(weight, src, h, m=P):
                return pe.matmul(ps[0:m, SM, :], weight, src[:, cols(h)], start=True, stop=True)

            def pair_product(weight, src):
                for h in range(2):
                    mm = pe.matmul(ps[:, pair_bank(h), :], weight, src[:, cols(h)], start=True, stop=True)
                return mm

            def small_product(name):
                start_small(name)
                if name.startswith("turn"):
                    _, f, u = name.split("_")
                    u = int(u)
                    pe.wait_ge(max_ready[f], u - FAMILIES[f][2] + 1)
                    mm = pe.transpose(ps[0:NT, SM, 0:P], negmax[:, u, :], w("ident"))
                elif name.startswith("sum"):
                    f = int(name[3:])
                    pe.wait_ge(o_taken[0], f + 1)
                    mm = pe.matmul(ps[:, SM, :], w("spread_sum"), oatt[:, f, :], start=True, stop=True)
                elif name in ("pre", "norm", "post"):
                    pe.wait_ge(done[f"{name}_stats"], 1)
                    mm = pe.matmul(ps[:, SM, 0:2], w("group"), mv[:, 0, :], start=True, stop=True)
                elif name in ("kA0", "kA1", "qA0", "qA1"):
                    pe.wait_ge(done["xh_a"], 1)
                    mm = half_product(w("w" + name[0]), xh, int(name[2]))
                elif name in ("vA0", "vA1", "vm0", "vm1"):
                    h = int(name[2])
                    for t in range(4):
                        tt = 4 * h + t
                        mm = pe.matmul(ps[:, SM, t * P:(t + 1) * P], xh[:, tt * P:(tt + 1) * P],
                                       w("wv" if name[1] == "A" else "wvm"), start=True, stop=True)
                elif name in ("c10", "c11"):
                    pe.wait_ge(done["x1"], 1)
                    mm = half_product(sa1w[:, :], x1, int(name[2]), 96)
                elif name in ("c20", "c21"):
                    h = int(name[2])
                    pe.wait_ge(done["conv_in"], 2)
                    for dy in range(3):
                        mm = pe.matmul(ps[0:HD, SM, :], sa2w[:, dy, :],
                                       conv_in[:, 16 * h + dy:16 * h + dy + 16, :].rearrange("p y x -> p (y x)"),
                                       start=(dy == 0), stop=(dy == 2))
                elif name in ("c30", "c31"):
                    pe.wait_ge(done["conv2"], 1 + int(name[2]))
                    mm = half_product(sa3w[:, :], conv2, int(name[2]))
                elif name.startswith("km"):
                    mm = half_product(w(f"wkm{name[2]}"), xh, int(name[3]))
                elif name.startswith("qm"):
                    mm = half_product(w(f"wqm{name[2]}"), gated, int(name[3]))
                elif name.startswith("tro"):
                    f = int(name[3:])
                    mm = transposes(SM, lambda t: oatt[:, f, t * P:(t + 1) * P])
                elif name.startswith("trn"):
                    h = int(name[3:])
                    pe.wait_ge(done["ln_e"], 1)
                    mm = transposes(SM, lambda t: lnt[:, 4 * h + t, :])
                elif name == "logits":
                    pe.wait_ge(done["xe"], 2)
                    for t in range(NT):
                        mm = pe.matmul(ps[:, SM, t * NE:(t + 1) * NE], xe[:, t * P:(t + 1) * P], gww[:, :],
                                       start=True, stop=True)
                elif name.startswith("trg"):
                    h = int(name[3:])
                    pe.wait_ge(done["gates"], 1)
                    mm = transposes(SM, lambda t: gate[:, 4 * h + t, :], rows=NE)
                elif name.startswith("b2"):
                    h = int(name[2:])
                    pe.wait_ge(done["gate_t"], 1 + h)
                    for t in range(4):
                        tt = 4 * h + t
                        mm = pe.matmul(ps[:, SM, t * P:(t + 1) * P], gate_t[:, tt * P:(tt + 1) * P], b2w[:, :],
                                       start=True, stop=True)
                elif name == "ff1":
                    pe.wait_ge(o_scaled[0], 4)
                    pe.wait_ge(mo_scaled, 2)
                    for q in range(2):
                        bank = ps[:, pair_bank(q), :]
                        pe.matmul(bank, w("ffa0"), oatt[:, q, :], start=True, stop=False)
                        pe.matmul(bank, w("ffa1"), oatt[:, 2 + q, :], start=False, stop=False)
                        mm = pe.matmul(bank, w("ffb"), omul[:, cols(q)], start=False, stop=True)
                elif name == "ff2":
                    pe.wait_ge(done["ff_act"], 1)
                    mm = pair_product(w("ff2"), tb)
                elif name == "outp":
                    pe.wait_ge(done["ff2"], 1)
                    mm = pair_product(w("out"), ta)
                elif name == "tr_x":
                    pe.wait_ge(done["xr"], 1)
                    for h in range(2):
                        mm = transposes(pair_bank(h), lambda t: x1[:, (4 * h + t) * P:(4 * h + t + 1) * P])
                elif name == "tr_nb":
                    pe.wait_ge(done["ln_b"], 1)
                    for h in range(2):
                        mm = transposes(pair_bank(h), lambda t: lnt[:, 4 * h + t, :])
                elif name in ("kB", "qB"):
                    pe.wait_ge(done["xh_b"], 1)
                    mm = pair_product(w(f"w{name}"), xh)
                elif name == "vB":
                    for t in range(NT):
                        mm = pe.matmul(ps[:, pair_bank(t // 4), (t % 4) * P:(t % 4 + 1) * P], xh[:, t * P:(t + 1) * P],
                                       w("wvB"), start=True, stop=True)
                mm.then_inc(small_full, 1)

            def scores(a, n, pr):
                g, q, t = n // STEPS, n // NT % 2, n % NT
                if n % STEPS == 0 and pr == 0 and (a, g) != (0, 0):
                    f = "a1" if a == 0 else "b"
                    pe.wait_ge(rows_in[f], 16 * GH * (1 if a == 0 else g + 1))
                if n >= 1:
                    pe.wait_ge(exp_done[a], 2 * (n - 1) + pr + 1)
                elif a == 1:
                    pe.wait_ge(y_used, UNITS)
                    pe.wait_ge(result, 2)
                for j in range(2):
                    h = 2 * pr + j
                    mm = pe.matmul(ps[:, SC + h, :], ks[:, slot_of(a, g), h, t * P:(t + 1) * P],
                                   qs[:, slot_of(a, g), h, cols(q)], start=True, stop=True)
                mm.then_inc(scores_ready[a], 1)

            def weigh_values(a, n):
                g, t = n // STEPS, n % NT
                pe.wait_ge(exp_done[a], 2 * n + 2)
                if t == 0 and n:
                    pe.wait_ge(o_taken[a], n // NT)
                if a == 1 and n == 0:
                    pe.wait_ge(done["v_b"], 1)
                for j in range(GH):
                    mm = pe.matmul(ps[32 * j:32 * j + 32, OB, :], va[a][:, t, GH * g + j, :], prob[:, n % 3, j, :],
                                   start=(t == 0), stop=(t == NT - 1))
                mm.then_inc(pv_done[a], 1)

            def attention_step(a, n, blocks, run):
                for f, j in blocks[0:1]:
                    max_block(f, j)
                if run:
                    scores(a, n, 0)
                for f, j in blocks[1:2]:
                    max_block(f, j)
                if run:
                    scores(a, n, 1)
                for f, j in blocks[2:3]:
                    max_block(f, j)
                if run and n:
                    weigh_values(a, n - 1)
                for f, j in blocks[3:]:
                    max_block(f, j)

            if experts:
                for n in range(2 * STEPS):
                    blocks = [("a1", j) for j in conv_blocks(n)] if conv else []
                    attention_step(0, n, blocks, conv)
                    for name in CONV_WINDOW.get(n, ()):
                        if conv or for_last_norm(name):
                            small_product(name)

            if conv:
                pe.wait_ge(rows_in["a1"], 16 * (GH + MULTI))
                for n in range(STEPS + 1):
                    if n < STEPS:
                        q, t = n // NT, n % NT
                        if n >= 2:
                            pe.wait_ge(mexp_done, n - 1)
                        else:
                            pe.wait_ge(exp_done[0], 4 * STEPS)
                        for m in range(MULTI):
                            mm = pe.matmul(ps[:, SC + 2 * (n % 2) + m, :], km[:, m, t * P:(t + 1) * P],
                                           qm[:, m, cols(q)], start=True, stop=True)
                        mm.then_inc(ms_ready, 1)
                    if n == 0:
                        weigh_values(0, 2 * STEPS - 1)
                    if n >= 1:
                        q, t = (n - 1) // NT, (n - 1) % NT
                        if n == 1:
                            pe.wait_ge(o_taken[0], 4)
                            pe.wait_ge(blocks_used["a1"], 96)
                        if n == NT + 1:
                            pe.wait_ge(mo_taken, 1)
                        pe.wait_ge(mexp_done, n)
                        for m in range(MULTI):
                            pe.matmul(ps[MD * m:MD * (m + 1), OB, :], vm[:, t, MD * m:MD * (m + 1)],
                                      prob[:, (n - 1) % 3, m, :], start=(t == 0), stop=(t == NT - 1))
                        for m in range(MULTI):
                            mm = pe.matmul(ps[MD * m:MD * (m + 1), MX + q, :], w("ones")[:, 0:MD],
                                           prob[:, (n - 1) % 3, m, :], start=(t == 0), stop=(t == NT - 1))
                        mm.then_inc(mpv_done, 1)
                    for name in PARTS_WINDOW.get(n, ()):
                        small_product(name)

            def hidden(u):
                e, h = u // 2, u % 2
                if h == 0:
                    pe.wait_ge(weights_ready, 32 * (e + 1))
                for c in range(NC):
                    n = NC * u + c
                    if n >= 2:
                        pe.wait_ge(gelu_done, n - 1)
                    elif conv:
                        pe.wait_ge(mexp_done, STEPS)
                    pe.matmul(ps[:, SC + n % 2, :], w1e[e % 2][:, c * P:(c + 1) * P], xe[:, cols(h)],
                              start=True, stop=True).then_inc(hid_ready, 1)

            def expert_out(u):
                e = u // 2
                pe.wait_ge(gelu_done, NC * (u + 1))
                if u >= 2:
                    pe.wait_ge(y_used, u - 1)
                for t in range(4):
                    for c in range(NC):
                        mm = pe.matmul(ps[:, SC + 2 + u % 2, t * P:(t + 1) * P], prob[:, u % 2, c, t * P:(t + 1) * P],
                                       w2e[e % 2][:, c * P:(c + 1) * P], start=(c == 0), stop=(c == NC - 1))
                mm.then_inc(y_ready, 1)

            if experts:
                for s in range(2 * UNITS + 2):
                    if s % 2 == 0 and s // 2 < UNITS:
                        hidden(s // 2)
                    if s % 2 == 1 and s >= 3:
                        expert_out((s - 3) // 2)
                    if token:
                        for name in EXPERT_WINDOW.get(s, ()):
                            if name == "ff1":
                                pe.wait_ge(mo_taken, 2)
                            small_product(name)
                        for j in expert_blocks(s):
                            max_block("b", j)
                pe.wait_ge(y_used, UNITS)
                for h in range(2):
                    transposes(SC + h, lambda t: toke[:, 4 * h + t, :]).then_inc(result_ready, 1)

            if front:
                for n in range(2 * STEPS):
                    blocks = ([("b", j) for j in token_blocks(n)] if token else []) + [("a0", j) for j in front_blocks(n)]
                    attention_step(1, n, blocks, token)
                    for name in TOKEN_WINDOW.get(n, ()):
                        if token or for_front(name):
                            small_product(name)
                if token:
                    weigh_values(1, 2 * STEPS - 1)

        def scalar_program(act, conv, experts, token, front, small):
            def read_small(dst, src, name, event, func=ACT.Copy, free=False, **kw):
                act.wait_ge(small_full, small[name])
                act.activation(dst, src, func, **kw).then_inc(small_free if free else done[event], 1)

            def small_product(name):
                if name in ("kA0", "kA1", "qA0", "qA1"):
                    i, h = "kq".index(name[0]), int(name[2])
                    read_small(parts[:, i, 0, cols(h)], ps[:, SM, :], name, f"{name[0]}1_a")
                elif name in ("c10", "c11"):
                    read_small(ta[0:96, cols(int(name[2]))], ps[0:96, SM, :], name, "tanh1", ACT.Tanh,
                               bias=half_b[0:96, 1:2], scale=0.5)
                elif name in ("c20", "c21"):
                    read_small(ta[0:HD, cols(int(name[2]))], ps[0:HD, SM, :], name, "tanh2", ACT.Tanh,
                               bias=half_b[0:HD, 2:3], scale=0.5)
                elif name in ("c30", "c31"):
                    read_small(ta[:, cols(int(name[2]))], ps[:, SM, :], name, "tanh3", ACT.Tanh,
                               bias=half_b[:, 3:4], scale=0.5)
                elif name in ("vm0", "vm1"):
                    h = int(name[2])
                    read_small(vm[:, 4 * h:4 * h + 4, :].rearrange("p t c -> p (t c)"), ps[:, SM, :], name, "", free=True)
                elif name.startswith("km"):
                    read_small(km[0:MD, int(name[2]), cols(int(name[3]))], ps[0:MD, SM, :], name, "km")
                elif name.startswith("qm"):
                    read_small(qm[0:MD, int(name[2]), cols(int(name[3]))], ps[0:MD, SM, :], name, "qm", scale=0.5)
                elif name.startswith("trn"):
                    read_small(xe[:, cols(int(name[3:]))], ps[:, SM, :], name, "xe")
                elif name == "ff1":
                    read_small(two(ta[:, :]), pair(), name, "tanh_ff", ACT.Tanh, bias=half_b[:, 0:1], scale=0.5)
                elif name == "ff2":
                    read_small(two(ta[:, :]), pair(), name, "ff2", ACT.Identity, bias=v("ff_b2"))
                elif name == "outp":
                    read_small(two(tb[:, :]), pair(), name, "outp", ACT.Identity, bias=v("out_b"))
                elif name == "tr_x":
                    read_small(tok[:, :, :].rearrange("p (a t) c -> p a (t c)", a=2), pair(), name, "tok")
                elif name == "tr_nb":
                    read_small(two(xh[:, :]), pair(), name, "xh_b")
                elif name in ("kB", "qB"):
                    i = "kq".index(name[0])
                    read_small(two(parts[:, i, 0, :]), pair(), name, f"{name[0]}1_b")
                    act.wait_ge(done[f"{name[0]}_rem_b"], 1)
                    act.activation(parts[:, i, 1, :], rem[:, :], ACT.Copy).then_inc(done[f"{name[0]}2_b"], 1)

            def second_part(name):
                i, h = "kq".index(name[0]), int(name[2])
                act.wait_ge(done[f"{name[0]}_rem_a"], h + 1)
                act.activation(parts[:, i, 1, cols(h)], rem[:, cols(h)], ACT.Copy).then_inc(done[f"{name[0]}2_a"], 1)

            def exps(a, n):
                if n >= 3:
                    act.wait_ge(pv_done[a], n - 2)
                for pr in range(2):
                    act.wait_ge(scores_ready[a], 2 * n + pr + 1)
                    act.activation(prob[:, n % 3, 2 * pr:2 * pr + 2, :], ps[:, SC + 2 * pr:SC + 2 * pr + 2, :], ACT.Exp,
                                   scale=HD ** -0.5).then_inc(exp_done[a], 1)

            if experts:
                for n in range(2 * STEPS):
                    if conv:
                        exps(0, n)
                    for name in CONV_WINDOW.get(n, ()):
                        if conv or for_last_norm(name):
                            small_product(name)
                    if n == 10:
                        act.wait_ge(done["gate_diff"], 1)
                        act.activation(ex[:, :, :], logit[:, :, :], ACT.Exp).then_inc(done["gate_exp"], 1)
            if conv:
                act.wait_ge(pv_done[0], 2 * STEPS)
                for n in range(STEPS):
                    if n >= 3:
                        act.wait_ge(mpv_done, n - 2)
                    act.wait_ge(ms_ready, n + 1)
                    act.activation(prob[:, n % 3, 0:2, :], ps[:, SC + 2 * (n % 2):SC + 2 * (n % 2) + 2, :], ACT.Exp,
                                   scale=MD ** -0.5).then_inc(mexp_done, 1)
                act.wait_ge(mpv_done, STEPS)
            if experts:
                for s in range(2 * UNITS + 2):
                    u = s // 2
                    if s % 2 == 0 and u < UNITS:
                        if u >= 2:
                            act.wait_ge(y_ready, u - 1)
                        for c in range(NC):
                            n = NC * u + c
                            act.wait_ge(hid_ready, n + 1)
                            act.activation(prob[:, u % 2, c, :], ps[:, SC + n % 2, :], ACT.Gelu,
                                           bias=b1w[:, u // 2, c:c + 1]).then_inc(gelu_done, 1)
                    if token:
                        for name in EXPERT_WINDOW.get(s, ()):
                            small_product(name)
                for h in range(2):
                    act.wait_ge(result_ready, h + 1)
                    act.activation(xe[:, cols(h)], ps[:, SC + h, :], ACT.Copy).then_inc(result, 1)
            if front:
                for n in range(2 * STEPS):
                    if token:
                        if n == 0:
                            act.wait_ge(y_ready, UNITS)
                        exps(1, n)
                    for name in TOKEN_WINDOW.get(n - 1, ()):
                        if name in ("kA0", "kA1", "qA0", "qA1"):
                            second_part(name)
                    for name in TOKEN_WINDOW.get(n, ()):
                        if token or for_front(name):
                            small_product(name)

        def vector_program(dve, conv, experts, token, front, small):
            chain = [0]

            def note(ins):
                chain[0] += 1
                ins.then_inc(dve_chain, 1)

            def sync():
                dve.wait_ge(dve_chain, chain[0])

            def link(ins):
                note(ins)
                sync()

            def read_small(name):
                dve.wait_ge(small_full, small[name])

            def freed(name):
                dve.wait_ge(small_free, small[name])

            def group_stats(src, name):
                for h in range(2):
                    note(dve.bn_stats(st[:, h, :], src[:, cols(h)]))
                sync()
                link(dve.bn_aggr(mv[:, 0, :], st[:, 0:2, :]))
                dve.scalar_tensor_tensor(out=mv[:, 0, 1:2], in0=mv[:, 0, 0:1], scalar=mv[:, 0, 0:1],
                                         in1=mv[:, 0, 1:2], op0=ALU.mult, op1=ALU.add).then_inc(done[f"{name}_stats"], 1)

            def group_var(name):
                read_small(name)
                dve.tensor_copy(gs[:, :], ps[:, SM, 0:2]).then_inc(small_free, 1)
                freed(name)
                link(dve.tensor_tensor(nb[:, 0:1], gs[:, 0:1], gs[:, 0:1], ALU.mult))
                link(dve.scalar_tensor_tensor(out=vn[:, 0:1], in0=nb[:, 0:1], scalar=-1.0, in1=gs[:, 1:2],
                                              op0=ALU.mult, op1=ALU.add))
                dve.tensor_scalar(vn[:, 0:1], vn[:, 0:1], 0.0, EPS_GN, ALU.max, ALU.add).then_inc(done[f"{name}_var"], 1)

            def group_coefs(name):
                dve.wait_ge(done[f"{name}_rstd"], 1)
                link(dve.tensor_tensor(ca[:, :], rs[:, 0:1], v(f"{name}_g"), ALU.mult))
                link(dve.tensor_tensor(nb[:, 0:1], gs[:, 0:1], ca[:, :], ALU.mult))
                link(dve.tensor_tensor(cb[:, :], v(f"{name}_b"), nb[:, 0:1], ALU.subtract))

            def layer_stats(src, name):
                for t in range(NT):
                    note(dve.bn_stats(st[:, t, :], src[:, t, :]))
                sync()
                for t in range(NT):
                    note(dve.bn_aggr(mv[:, t, :], st[:, t, :]))
                sync()
                dve.tensor_scalar(vn[:, :], mv[:, :, 1], 0.0, EPS_LN, ALU.max, ALU.add
                                  ).then_inc(done[f"ln_var_{name}"], 1)

            def layer_norm(src, name):
                dve.wait_ge(done[f"ln_rstd_{name}"], 1)
                link(dve.scalar_tensor_tensor(out=nb[:, :], in0=mv[:, :, 0], scalar=-1.0, in1=rs[:, :],
                                              op0=ALU.mult, op1=ALU.mult))
                for t in range(NT):
                    ins = dve.tensor_scalar(lnt[:, t, :], src[:, t, :], rs[:, t:t + 1], nb[:, t:t + 1],
                                            ALU.mult, ALU.add)
                    if t < NT - 1:
                        note(ins)
                ins.then_inc(done[f"ln_{name}"], 1)

            def reduce_block(f, j):
                a, first, first_unit = FAMILIES[f]
                u, t, k = block_of(j)
                n = j - first
                dve.wait_ge(blocks_ready[f], n + 1)
                dve.tensor_reduce(blockmax[:, u, t, k:k + 1], ps[:, MX + n % 2, :], AX.X, ALU.max
                                  ).then_inc(blocks_used[f], 1)
                if j % 16 == 15:
                    dve.wait_ge(blocks_used[f], n + 1)
                    dve.tensor_reduce(negmax[:, u, :], blockmax[:, u, :, :], AX.X, ALU.max, negate=True
                                      ).then_inc(max_ready[f], 1)

            def split_max(name):
                _, f, u = name.split("_")
                u = int(u)
                n = u - FAMILIES[f][2] + 1
                read_small(name)
                src = ps[0:NT, SM, 0:P]
                if u >= NH:
                    dve.tensor_copy(rowrem[:, :], src).then_inc(small_free, 1)
                    freed(name)
                    dve.tensor_copy(maxrow_m[:, u - NH, :], rowrem[:, :]).then_inc(rows_split[f], 1)
                    dve.wait_ge(rows_split[f], n)
                    return
                if n >= 3:
                    dve.wait_ge(rows_out[f], 16 * (n - 2))
                row = maxrow[:, u % 2, :, :]
                link(dve.tensor_copy(row[:, 0, :], src))
                dve.tensor_tensor(rowrem[:, :], src, row[:, 0, :], ALU.subtract).then_inc(small_free, 1)
                freed(name)
                link(dve.tensor_copy(row[:, 1, :], rowrem[:, :]))
                dve.tensor_tensor(row[:, 2, :], rowrem[:, :], row[:, 1, :], ALU.subtract).then_inc(rows_split[f], 1)
                dve.wait_ge(rows_split[f], n)

            def take_output(a, f):
                dve.wait_ge(pv_done[a], NT * (f + 1))
                dve.tensor_copy(oatt[:, f, :], ps[:, OB, :]).then_inc(o_taken[a], 1)

            def take_values(a, h, src):
                return dve.tensor_copy(va[a][:, 4 * h:4 * h + 4, :, 0:HD], src.rearrange("p (t h d) -> p t h d", t=4, h=NH))

            def third_part(name):
                i, h = "kq".index(name[0]), int(name[2])
                dve.wait_ge(done[f"{name[0]}2_a"], h + 1)
                dve.tensor_tensor(parts[:, i, 2, cols(h)], rem[:, cols(h)], parts[:, i, 1, cols(h)], ALU.subtract
                                  ).then_inc(done[f"{name[0]}3_a"], 1)

            def small_product(name):
                h = int(name[-1]) if name[-1].isdigit() else 0
                if name.startswith("turn"):
                    split_max(name)
                elif name.startswith("sum"):
                    return
                elif name in ("pre", "norm"):
                    group_var(name)
                elif name in ("kA0", "kA1", "qA0", "qA1"):
                    i = "kq".index(name[0])
                    dve.wait_ge(done[f"{name[0]}1_a"], h + 1)
                    if i == 1:
                        dve.wait_ge(done["k3_a"], h + 1)
                    dve.tensor_tensor(rem[:, cols(h)], ps[:, SM, :], parts[:, i, 0, cols(h)], ALU.subtract
                                      ).then_inc(small_free, 1)
                    freed(name)
                    dve.sem_inc(done[f"{name[0]}_rem_a"], 1)
                elif name in ("vA0", "vA1"):
                    read_small(name)
                    take_values(0, h, ps[:, SM, :]).then_inc(small_free, 1)
                elif name in ("c10", "c11"):
                    dve.wait_ge(done["tanh1"], h + 1)
                    dve.tensor_scalar(tb[0:96, cols(h)], ps[0:96, SM, :], v("sa_b1", 96), 0.5, ALU.add, ALU.mult
                                      ).then_inc(small_free, 1)
                    freed(name)
                    for dx in range(3):
                        qd = slice(32 * dx, 32 * dx + 32)
                        lo, hi = max(0, 1 - dx), min(SIDE, SIDE + 1 - dx)

                        def shifted(ap):
                            return ap[qd, cols(h)].rearrange("p (y x) -> p y x", x=SIDE)[:, :, lo + dx - 1:hi + dx - 1]

                        ins = dve.scalar_tensor_tensor(out=conv_in[qd, 1 + 16 * h:17 + 16 * h, lo:hi], in0=shifted(ta),
                                                       scalar=1.0, in1=shifted(tb), op0=ALU.add, op1=ALU.mult)
                        if dx < 2:
                            note(ins)
                    ins.then_inc(done["conv_in"], 1)
                    sync()
                elif name in ("c20", "c21"):
                    dve.wait_ge(done["tanh2"], h + 1)
                    dve.tensor_scalar(tb[0:HD, cols(h)], ps[0:HD, SM, :], v("sa_b2", HD), 0.5, ALU.add, ALU.mult
                                      ).then_inc(small_free, 1)
                    freed(name)
                    dve.scalar_tensor_tensor(out=conv2[:, cols(h)], in0=ta[0:HD, cols(h)], scalar=1.0,
                                             in1=tb[0:HD, cols(h)], op0=ALU.add, op1=ALU.mult
                                             ).then_inc(done["conv2"], 1)
                elif name in ("c30", "c31"):
                    dve.wait_ge(done["tanh3"], h + 1)
                    dve.scalar_tensor_tensor(out=gated[:, cols(h)], in0=ta[:, cols(h)], scalar=1.0, in1=x1[:, cols(h)],
                                             op0=ALU.add, op1=ALU.mult).then_inc(small_free, 1)
                elif name.startswith("km"):
                    m = int(name[2])
                    dve.wait_ge(done["km"], 2 * m + h + 1)
                    dve.tensor_copy(kmh[:, m, cols(h)], ps[:, SM, :]).then_inc(small_free, 1)
                    freed(name)
                    dve.sem_inc(done["kmh"], 1)
                elif name.startswith("qm"):
                    m = int(name[2])
                    dve.wait_ge(done["qm"], 2 * m + h + 1)
                    link(dve.tensor_scalar(qmh[:, m, cols(h)], ps[:, SM, :], 0.5, None, ALU.mult))
                    dve.scalar_tensor_tensor(out=qmh[MD:P, m, cols(h)], in0=ps[MD:P, SM, :], scalar=0.5,
                                             in1=qmh[MD:P, m, cols(h)], op0=ALU.mult, op1=ALU.subtract
                                             ).then_inc(small_free, 1)
                    freed(name)
                    dve.sem_inc(done["qmh"], 1)
                elif name.startswith("tro"):
                    g, q = h // 2, h % 2
                    read_small(name)
                    o = ps[:, SM, :].rearrange("p (t j r) -> p t j r", t=4, r=2 * HD)
                    link(dve.reciprocal(orec[:, :, :], o[:, :, :, HD]))
                    oview = rec[:, 0:4 * GH * HD].rearrange("p (t j d) -> p t j d", t=4, d=HD)
                    dve.tensor_tensor(oview, o[:, :, :, 0:HD], orec[:, :, :].unsqueeze(3).to_broadcast([P, 4, GH, HD]),
                                      ALU.mult).then_inc(small_free, 1)
                    freed(name)
                    c = slice(GH * HD * g, GH * HD * (g + 1))
                    link(dve.tensor_tensor(toke[:, 4 * q:4 * q + 4, c], tok[:, 4 * q:4 * q + 4, c],
                                           rec[:, 0:4 * GH * HD].rearrange("p (t c) -> p t c", t=4), ALU.add))
                elif name == "logits":
                    read_small(name)
                    dve.tensor_tensor(logit[:, :, :], ps[:, SM, 0:NT * NE].rearrange("p (t e) -> p t e", t=NT),
                                      gbw[:, :, :], ALU.add).then_inc(small_free, 1)
                    freed(name)
                    for t in range(NT):
                        note(dve.max(top[:, t, :], logit[:, t, :]))
                    sync()
                    for t in range(NT):
                        note(dve.max_index(topi[:, t, :], top[:, t, :], logit[:, t, :]))
                    sync()
                    link(dve.tensor_copy(topf[:, :, :], topi[:, :, 0:2]))
                    dve.tensor_tensor(logit[:, :, :], logit[:, :, :], top[:, :, 0:1].to_broadcast([P, NT, NE]),
                                      ALU.subtract).then_inc(done["gate_diff"], 1)
                elif name.startswith("trg"):
                    read_small(name)
                    dve.tensor_copy(gate_t[:, cols(h)], ps[0:NE, SM, :]).then_inc(small_free, 1)
                    freed(name)
                    dve.sem_inc(done["gate_t"], 1)
                elif name.startswith("b2"):
                    read_small(name)
                    tv = toke[:, 4 * h:4 * h + 4, :].rearrange("p t c -> p (t c)")
                    dve.tensor_tensor(tv, tv, ps[:, SM, :], ALU.add).then_inc(small_free, 1)
                    freed(name)
                elif name == "ff1":
                    dve.wait_ge(done["tanh_ff"], 1)
                    dve.tensor_scalar(two(tb[:, :]), pair(), v("ff_b1"), 0.5, ALU.add, ALU.mult).then_inc(small_free, 1)
                    freed(name)
                    dve.scalar_tensor_tensor(out=tb[:, :], in0=ta[:, :], scalar=1.0, in1=tb[:, :],
                                             op0=ALU.add, op1=ALU.mult).then_inc(done["ff_act"], 1)
                elif name == "outp":
                    dve.wait_ge(done["outp"], 1)
                    dve.sem_inc(small_free, 1)
                    group_stats(tb, "post")
                elif name == "post":
                    group_var("post")
                    group_coefs("post")
                    link(dve.scalar_tensor_tensor(out=x1[:, :], in0=tb[:, :], scalar=ca[:, :], in1=xin[:, :],
                                                  op0=ALU.mult, op1=ALU.add))
                    dve.tensor_scalar(x1[:, :], x1[:, :], cb[:, :], None, ALU.add).then_inc(done["xr"], 1)
                elif name == "tr_x":
                    dve.wait_ge(done["tok"], 1)
                    dve.sem_inc(small_free, 1)
                    layer_stats(tok, "b")
                    layer_norm(tok, "b")
                elif name in ("ff2", "tr_nb"):
                    dve.wait_ge(done[{"ff2": "ff2", "tr_nb": "xh_b"}[name]], 1)
                    dve.sem_inc(small_free, 1)
                elif name.startswith("trn"):
                    dve.wait_ge(done["xe"], h + 1)
                    dve.sem_inc(small_free, 1)
                elif name in ("kB", "qB"):
                    i = "kq".index(name[0])
                    dve.wait_ge(done[f"{name[0]}1_b"], 1)
                    if i == 1:
                        dve.wait_ge(done["k3_b"], 1)
                    dve.tensor_tensor(two(rem[:, :]), pair(), two(parts[:, i, 0, :]), ALU.subtract).then_inc(small_free, 1)
                    freed(name)
                    dve.sem_inc(done[f"{name[0]}_rem_b"], 1)
                    dve.wait_ge(done[f"{name[0]}2_b"], 1)
                    dve.tensor_tensor(parts[:, i, 2, :], rem[:, :], parts[:, i, 1, :], ALU.subtract
                                      ).then_inc(done[f"{name[0]}3_b"], 1)
                elif name == "vB":
                    read_small(name)
                    for hh in range(2):
                        ins = take_values(1, hh, ps[:, pair_bank(hh), :])
                        if hh == 0:
                            note(ins)
                    ins.then_inc(small_free, 1)
                    freed(name)
                    dve.sem_inc(done["v_b"], 1)

            def scale_output(f):
                name = f"sum{f}"
                read_small(name)
                dve.reciprocal(rec[:, :], ps[:, SM, :]).then_inc(small_free, 1)
                freed(name)
                dve.tensor_tensor(oatt[:, f, :], oatt[:, f, :], rec[:, :], ALU.mult).then_inc(o_scaled[0], 1)
                dve.wait_ge(o_scaled[0], f + 1)

            def gates():
                link(dve.tensor_tensor(oh[:, :, :], iow[:, :, :], topf[:, :, 0:1].to_broadcast([P, NT, NE]),
                                       ALU.is_equal))
                link(dve.tensor_tensor(gate[:, :, :], iow[:, :, :], topf[:, :, 1:2].to_broadcast([P, NT, NE]),
                                       ALU.is_equal))
                link(dve.tensor_tensor(gate[:, :, :], gate[:, :, :], oh[:, :, :], ALU.add))
                dve.wait_ge(done["gate_exp"], 1)
                link(dve.tensor_reduce(esum[:, :], ex[:, :, :], AX.X, ALU.add))
                link(dve.reciprocal(erec[:, :], esum[:, :]))
                link(dve.tensor_tensor(gate[:, :, :], gate[:, :, :], ex[:, :, :], ALU.mult))
                dve.tensor_tensor(gate[:, :, :], gate[:, :, :], erec[:, :].unsqueeze(2).to_broadcast([P, NT, NE]),
                                  ALU.mult).then_inc(done["gates"], 1)
                dve.wait_ge(done["gates"], 1)

            def attention_step(a, n, blocks, run):
                for f, j in blocks[0:3]:
                    reduce_block(f, j)
                if run and n and n % NT == 0:
                    take_output(a, n // NT - 1)
                for f, j in blocks[3:]:
                    reduce_block(f, j)

            if experts:
                for n in range(2 * STEPS):
                    blocks = [("a1", j) for j in conv_blocks(n)] if conv else []
                    attention_step(0, n, blocks, conv)
                    if n == 4:
                        layer_stats(toke, "e")
                    if n == 5:
                        layer_norm(toke, "e")
                    if conv and n >= 11 and n % NT == 3:
                        scale_output(n // NT - 1)
                    if n == 11:
                        gates()
                    for name in CONV_WINDOW.get(n, ()):
                        if conv or for_last_norm(name):
                            small_product(name)
            if conv:
                for q in range(2):
                    if q == 0:
                        take_output(0, 3)
                        scale_output(3)
                    dve.wait_ge(mpv_done, NT * (q + 1))
                    dve.tensor_copy(tb[:, cols(0)], ps[:, OB, :]).then_inc(mo_taken, 1)
                    dve.wait_ge(mo_taken, q + 1)
                    link(dve.reciprocal(rec[:, :], ps[:, MX + q, :]))
                    dve.tensor_tensor(omul[:, cols(q)], tb[:, cols(0)], rec[:, :], ALU.mult).then_inc(mo_scaled, 1)
                    dve.wait_ge(mo_scaled, q + 1)
            if experts:
                for s in range(2 * UNITS + 2):
                    if s % 2 == 1 and s >= 3:
                        u = (s - 3) // 2
                        e, h = u // 2, u % 2
                        dve.wait_ge(y_ready, u + 1)
                        if u >= 2:
                            dve.wait_ge(y_used, u - 1)
                            sync()
                        for t in range(4):
                            tt = 4 * h + t
                            ins = dve.scalar_tensor_tensor(out=toke[:, tt, :],
                                                           in0=ps[:, SC + 2 + u % 2, t * P:(t + 1) * P],
                                                           scalar=gate[:, tt, e:e + 1], in1=toke[:, tt, :],
                                                           op0=ALU.mult, op1=ALU.add)
                            if t < 3:
                                note(ins)
                        ins.then_inc(y_used, 1)
                    if token:
                        for name in EXPERT_WINDOW.get(s, ()):
                            small_product(name)
                        for j in expert_blocks(s):
                            reduce_block("b", j)
            if front:
                for n in range(2 * STEPS):
                    blocks = ([("b", j) for j in token_blocks(n)] if token else []) + [("a0", j) for j in front_blocks(n)]
                    attention_step(1, n, blocks, token)
                    if n == 0:
                        dve.wait_ge(x_in, 16)
                        group_stats(xin, "pre")
                    if n == 2:
                        group_coefs("pre")
                        link(dve.scalar_tensor_tensor(out=x1[:, :], in0=xin[:, :], scalar=ca[:, :], in1=posw[:, :],
                                                      op0=ALU.mult, op1=ALU.add))
                        dve.tensor_scalar(x1[:, :], x1[:, :], cb[:, :], None, ALU.add).then_inc(done["x1"], 1)
                        dve.wait_ge(done["x1"], 1)
                    if n == 3:
                        group_stats(x1, "norm")
                    if n == 6:
                        group_coefs("norm")
                        dve.tensor_scalar(xh[:, :], x1[:, :], ca[:, :], cb[:, :], ALU.mult, ALU.add
                                          ).then_inc(done["xh_a"], 1)
                    for name in TOKEN_WINDOW.get(n - 1, ()):
                        if name in ("kA0", "kA1", "qA0", "qA1"):
                            third_part(name)
                    for name in TOKEN_WINDOW.get(n, ()):
                        if token or for_front(name):
                            small_product(name)
                if token:
                    take_output(1, 3)

        def run_block(img, conv, experts, token, front, small):
            with nc.Block(no_gpsimd_drain=True) as block:
                @block.sync
                def _(sp):
                    sync_program(sp, img, conv, experts, token, front, small)

                @block.gpsimd
                def _(pool):
                    pool_program(pool, conv, experts, token, front, small)

                @block.tensor
                def _(pe):
                    tensor_program(pe, conv, experts, token, front, small)

                @block.scalar
                def _(act):
                    scalar_program(act, conv, experts, token, front, small)

                @block.vector
                def _(dve):
                    vector_program(dve, conv, experts, token, front, small)
            nc.all_engine_barrier(sems_to_clear=cleared)

        run_block(0, False, False, False, True, Small(only(TOKEN_WINDOW, for_front)))
        with nc.Fori(0, NB) as img:
            run_block(img, True, True, True, True, Small(CONV_WINDOW, PARTS_WINDOW, EXPERT_WINDOW, TOKEN_WINDOW))
        run_block(0, False, True, False, False, Small(only(CONV_WINDOW, for_last_norm)))


def kernel(**inputs):
    import numpy as np
    import concourse.bacc as bacc
    from concourse.bass_utils import run_bass_kernel_spmd

    g = {k: np.asarray(v) for k, v in inputs.items()}
    L0 = {k[len("L0_conv_"):]: v for k, v in g.items() if k.startswith("L0_conv_")}
    NB = g["x"].shape[0]
    f32 = np.float32

    eye = np.eye(P, dtype=f32)
    group = np.kron(np.eye(P // 4), np.full((4, 4), 0.25)).astype(f32)
    spread_sum = np.zeros((P, P), f32)
    for j in range(4):
        spread_sum[32 * j + HD, 32 * j:32 * j + 32] = 1.0

    def strips(wt, grp):
        o = np.zeros((P, P), f32)
        for j in range(4):
            o[32 * j:32 * j + HD] = wt[64 * grp + HD * j:64 * grp + HD * (j + 1)]
        return o

    ff1 = L0["ff_w1"].T
    qkv = g["L1_attn_w_qkv"]
    table = {
        "wk": L0["wk"].T, "wq": L0["wq"].T, "wv": L0["wv"].T,
        "wqB": qkv[:, 0:P], "wkB": qkv[:, P:2 * P], "wvB": qkv[:, 2 * P:],
        "ffa0": strips(ff1[:P], 0), "ffa1": strips(ff1[:P], 1), "ffb": ff1[P:],
        "ff2": L0["ff_w2"].T, "out": L0["out_w"].T,
        "wvm": np.concatenate([L0["wv0"].T, L0["wv1"].T], 1),
        "wkm0": np.concatenate([L0["wk0"].T] * 2, 1), "wkm1": np.concatenate([L0["wk1"].T] * 2, 1),
        "wqm0": np.concatenate([L0["wq0"].T] * 2, 1), "wqm1": np.concatenate([L0["wq1"].T] * 2, 1),
        "ident": eye, "group": group, "spread_sum": spread_sum, "ones": np.ones((P, P), f32),
    }

    def column(vals, at=(0,)):
        o = np.zeros(P, f32)
        for a in at:
            o[a:a + len(vals)] = vals
        return o

    vtable = {n: L0[n] for n in VECTORS if n in L0}
    vtable["sa_b1"] = column(L0["sa_b1"], (0, 32, 64))
    vtable["sa_b2"] = column(L0["sa_b2"])
    vtable["sa_b3"] = np.broadcast_to(L0["sa_b3"], (P,))
    vtable["neg_half"] = np.full(P, -0.5, f32)
    s1 = L0["sa_w1"].reshape(HD, P).T
    sa1 = np.zeros((P, 96), f32)
    sa2 = np.zeros((96, 3, HD), f32)
    for dx in range(3):
        sa1[:, 32 * dx:32 * dx + HD] = s1
        sa2[32 * dx:32 * dx + HD] = L0["sa_w2"][:, :, :, dx].transpose(1, 2, 0)
    arrays = {
        "x": g["x"].reshape(NB, P, S),
        "pos": L0["pos_emb"].reshape(P, S),
        "wts": np.stack([table[n] for n in WEIGHTS], 1),
        "vecs": np.stack([vtable[n] for n in VECTORS], 1),
        "sa1": sa1, "sa2": sa2,
        "sa3": np.repeat(L0["sa_w3"].reshape(HD, 1), P, 1),
        "w1": g["L1_ffn_w1"].transpose(1, 0, 2),
        "b1": g["L1_ffn_b1"].reshape(NE, NC, P).transpose(2, 0, 1),
        "w2": g["L1_ffn_w2"].reshape(NE, NC, P, P).transpose(2, 0, 1, 3).reshape(P, NE, HID),
        "b2": g["L1_ffn_b2"],
        "gw": g["L1_ffn_gate_w"],
        "gb": np.broadcast_to(g["L1_ffn_gate_b"], (P, NT, NE)),
        "iota": np.broadcast_to(np.arange(NE, dtype=f32), (P, NT, NE)),
    }
    nc = bacc.Bacc("TRN2", target_bir_lowering=False, num_devices=1)
    feed, args = {}, []
    for name, a in arrays.items():
        a = np.ascontiguousarray(a)
        feed[f"in_{name}"] = a
        args.append(nc.dram_tensor(f"in_{name}", a.shape, mybir.dt.from_np(a.dtype), kind="ExternalInput").ap())
    out = nc.dram_tensor("out_0", (NB, P, S), F32, kind="ExternalOutput").ap()
    build(nc, *args, out)
    r = run_bass_kernel_spmd(nc, [feed], core_ids=[0])
    return r.results[0]["out_0"].reshape(NB, P, SIDE, SIDE)
```

```python
from contextlib import ExitStack

import concourse.bass as bass
from concourse import mybir

F32 = mybir.dt.float32
BF16 = mybir.dt.bfloat16
U32 = mybir.dt.uint32
ACT = mybir.ActivationFunctionType
ALU = mybir.AluOpType
AX = mybir.AxisListType

P = 128
S = 1024
HALF = 512
NT = S // P
NH = 8
HD = P // NH
GH = 4
RUNS = (3, 2, 1)
PIECES = sum(RUNS)
ROWS = PIECES * HD
NE = 8
HID = 512
NC = HID // P
SIDE = 32
MULTI = 2
MD = 64
STEPS = 16
UNITS = 2 * NE
EPS_GN, EPS_LN = 1e-6, 1e-5

SC = 0
OB = 4
MX = 5
SM = 7

WEIGHTS = ["wk", "wq", "wv", "wkB", "wqB", "wvB", "ffa", "ffb", "ff2", "out",
           "wvm", "wkm0", "wkm1", "wqm0", "wqm1", "ident", "group", "ones"]
VECTORS = ["pre_g", "pre_b", "norm_g", "norm_b", "post_g", "post_b", "ff_b1", "ff_b2", "out_b",
           "sa_b1", "sa_b2", "sa_b3", "neg_half"]

A_FRONT = 72
FAMILIES = {"a0": (0, 0, A_FRONT, 0), "a1": (0, A_FRONT, 160, 4), "b": (1, 0, 128, 0)}

START_WINDOW = {0: ["pre"], 1: ["norm"]}
CONV_WINDOW = {0: ["tro0"], 1: ["km00"], 2: ["km01"], 3: ["qm00"], 4: ["qm01"], 5: ["km10"], 6: ["turn_a1_4"],
               7: ["km11"], 8: ["qm10"], 9: ["tra0"], 10: ["qm11"], 14: ["turn_a1_6", "tro1"], 15: ["tro2"],
               16: ["tro3"], 17: ["tra1"], 21: ["trn0"], 22: ["trn1"], 23: ["logits"], 25: ["tra2"],
               26: ["turn_a1_8"], 27: ["trg0"], 28: ["trg1"], 29: ["b20"], 30: ["b21"]}
CONV_EXTRA = {18: ["stats_e"], 20: ["norm_e"], 26: ["gates"]}
PARTS_WINDOW = {2: ["tra3"], 4: ["tob0"], 6: ["tob1"], 10: ["mtr0"], 12: ["mtb0"]}
EXPERT_WINDOW = {0: ["mtr1"], 1: ["mtb1"], 2: ["ff1"], 3: ["ff2"], 4: ["outp"], 5: ["post"], 7: ["tr_x"],
                 10: ["tr_nb"], 11: ["kB"], 12: ["qB"], 13: ["vB"], 15: ["pre"], 18: ["norm"], 24: ["turn_b_0"],
                 32: ["turn_b_2"]}
TOKEN_WINDOW = {0: ["kA0"], 1: ["kA1"], 2: ["qA0"], 3: ["qA1"], 4: ["vA0"], 5: ["vA1"], 6: ["turn_b_4"], 7: ["c10"],
                8: ["c11"], 10: ["vm0"], 13: ["c20"], 14: ["turn_b_6", "vm1"], 15: ["c21"], 17: ["c30"], 19: ["c31"],
                22: ["turn_a0_0"], 30: ["turn_a0_2"]}
LAST_NORM = ("tro", "trn", "logits", "trg", "b2")
SLOTS = 2 * UNITS + 2
B_START = 17
B_EARLY = 72


def blocks_at(n, at, steps, first, end):
    if not at <= n < at + steps:
        return range(0)
    return range(first + (end - first) * (n - at) // steps, first + (end - first) * (n - at + 1) // steps)


def conv_blocks(n):
    return [("a1", j) for j in blocks_at(n, 0, 14, A_FRONT, 128)] + [("a1", j) for j in blocks_at(n, 14, 11, 128, 160)]


def expert_blocks(s):
    return [("b", j) for j in blocks_at(s, B_START, SLOTS - B_START, 0, B_EARLY)]


def token_blocks(n, token):
    if not token:
        return [("a0", j) for j in blocks_at(n, 6, 18, 0, A_FRONT)]
    return [("b", j) for j in blocks_at(n, 0, 14, B_EARLY, 128)] + [("a0", j) for j in blocks_at(n, 14, 18, 0, A_FRONT)]


def block_of(j):
    return j // 16, j // 2 % NT, j % 2


def slot_of(a, g):
    return ((2, 0), (0, 1))[a][g]


def only(table, keep):
    return {n: kept for n, names in table.items() if (kept := [x for x in names if keep(x)])}


def for_front(name):
    return not name.startswith("turn_b")


def for_last_norm(name):
    return name.startswith(LAST_NORM)


class Small:

    def __init__(self, *windows):
        self.order = [x for w in windows for n in sorted(w) for x in w[n]]

    def __getitem__(self, name):
        return self.order.index(name) + 1


def build(nc, x, pos, wts, vecs, sa1, sa2, sa3, w1, b1, w2, b2, gw, gb, iota, out):
    NB = x.shape[0]
    ctx = ExitStack()
    with ctx:
        def sb(name, shape, dt=F32):
            return ctx.enter_context(nc.sbuf_tensor(name, shape, dt))

        def sem(name):
            return ctx.enter_context(nc.semaphore(name))

        ps = ctx.enter_context(nc.psum_tensor("ps", [P, 8, HALF], F32))

        wt = sb("wt", [P, len(WEIGHTS), P])
        vec = sb("vec", [P, len(VECTORS)])
        half_b = sb("half_b", [P, 4])
        posw = sb("posw", [P, S])
        sa1w = sb("sa1w", [P, 96])
        sa2w = sb("sa2w", [96, 3, HD])
        sa3w = sb("sa3w", [96, P])
        b1w = sb("b1w", [P, NE, NC])
        b2w = sb("b2w", [96, P])
        gww = sb("gww", [P, NE])
        gbw = sb("gbw", [P, NT, NE])
        iow = sb("iow", [P, NT, NE])

        def w(name):
            return wt[:, WEIGHTS.index(name), :]

        def v(name, n=P):
            i = VECTORS.index(name)
            return vec[0:n, i:i + 1]

        warm = sb("warm", [P, 1])
        xin = sb("xin", [P, S])
        x1 = sb("x1", [P, S])
        xh = sb("xh", [P, S])
        xe = sb("xe", [P, S])
        gated = sb("gated", [P, S])
        omul = gated
        ta = sb("ta", [P, S])
        tb = sb("tb", [P, S])
        conv_in = sb("conv_in", [96, SIDE + 2, SIDE])
        low = sb("low", [96, S])
        conv2, gate_t = low, low[0:NE, :]
        parts = sb("parts", [P, 2, 3, S], BF16)
        rem = ta
        ks = sb("ks", [ROWS + 3, 3, GH, S], BF16)
        qs = sb("qs", [ROWS + 3, 3, GH, S], BF16)
        va = [sb("va_a", [P, NT, NH, 2 * HD]),
              sb("va_b", [P, NT, NH, 2 * HD])]
        vm = sb("vm", [P, NT, P])
        km = sb("km", [MD + 1, MULTI, S])
        qm = sb("qm", [MD + 1, MULTI, S])
        shared = [sb("shared0", [P, 2, HALF]), sb("shared1", [P, 2, HALF])]
        kmh, qmh = (t[:, :, :].bitcast(BF16) for t in shared)
        w1e = [t[:, 0, :] for t in shared]
        w2e = [t[:, 1, :] for t in shared]
        prob = sb("prob", [P, 3, 4, HALF])
        oatt = sb("oatt", [P, 4, HALF])
        rec = tb[:, HALF:S]
        tok = sb("tok", [P, NT, P])
        toke = sb("toke", [P, NT, P])
        blockmax = sb("blockmax", [P, 10, NT, 2])
        negmax = sb("negmax", [P, 10, NT])
        maxrow = sb("maxrow", [2 * NT, 2, 3, P], BF16)
        maxrow_m = sb("maxrow_m", [2 * NT, P])
        rowrem = sb("rowrem", [2 * NT, P])
        st = sb("st", [P, NT, 6])
        mv = sb("mv", [P, NT, 2])
        gs = sb("gs", [P, 2])
        vn = sb("vn", [P, NT])
        rs = sb("rs", [P, NT])
        nb = sb("nb", [P, NT])
        ca = sb("ca", [P, 1])
        cb = sb("cb", [P, 1])
        orec = sb("orec", [P, 4, GH])
        logit = sb("logit", [P, NT, NE])
        top = sb("top", [P, NT, 8])
        topi = sb("topi", [P, NT, 8], U32)
        topf = sb("topf", [P, NT, 2])
        ex = sb("ex", [P, NT, NE])
        oh = sb("oh", [P, NT, NE])
        gate = sb("gate", [P, NT, NE])
        esum = sb("esum", [P, NT])
        erec = sb("erec", [P, NT])
        lnt = ta[:, :].rearrange("p (t c) -> p t c", t=NT)

        parts_dram = nc.dram_tensor("parts_dram", (2, 2, P, 3, S), BF16, kind="Internal").ap()
        maxrow_dram = nc.dram_tensor("maxrow_dram", (2, NH // 2, 2 * NT, 3, P), BF16, kind="Internal").ap()
        maxrow_m_dram = nc.dram_tensor("maxrow_m_dram", (MULTI * NT, P), F32, kind="Internal").ap()

        weights_in, consts_set, pool_set = sem("weights_in"), sem("consts_set"), sem("pool_set")

        x_in = sem("x_in")
        small_full, small_free = sem("small_full"), sem("small_free")
        dve_chain = sem("dve_chain")
        parts_out = [[sem("k_out_a"), sem("q_out_a")], [sem("k_out_b"), sem("q_out_b")]]
        spread = [[sem("spread_a0"), sem("spread_a1")], [sem("spread_b0"), sem("spread_b1")]]
        blocks_ready, blocks_used, max_ready, rows_split, rows_out, rows_in = (
            {f: sem(f"{n}_{f}") for f in FAMILIES}
            for n in ("blocks_ready", "blocks_used", "max_ready", "rows_split", "rows_out", "rows_in"))
        scores_ready, exp_done, pv_done, o_taken = (
            [sem(f"{n}_a"), sem(f"{n}_b")] for n in ("scores_ready", "exp_done", "pv_done", "o_taken"))
        ms_ready, mexp_done, mpv_done, mo_taken = (
            sem("ms_ready"), sem("mexp_done"), sem("mpv_done"), sem("mo_taken"))
        weights_ready, hid_ready, gelu_done = sem("weights_ready"), sem("hid_ready"), sem("gelu_done")
        y_ready, y_used, result_ready, result = sem("y_ready"), sem("y_used"), sem("result_ready"), sem("result")
        done = {name: sem(name) for name in (
            "pre_stats", "pre_var", "pre_rstd", "x1", "norm_stats", "norm_var", "norm_rstd", "xh_a",
            "k1_a", "k_rem_a", "k2_a", "k3_a", "q1_a", "q_rem_a", "q2_a", "q3_a",
            "tanh1", "conv_in", "tanh2", "conv2", "conv_in_dx", "gated",
            "qmh", "tanh_ff", "ff_act", "ff2", "outp", "post_stats", "post_var", "post_rstd",
            "xr", "tok", "ln_var_b", "ln_rstd_b", "ln_b", "xh_b",
            "k1_b", "k_rem_b", "k2_b", "k3_b", "q1_b", "q_rem_b", "q2_b", "q3_b", "v_b",
            "ln_var_e", "ln_rstd_e", "ln_e", "xe", "gate_diff", "gate_exp", "gates", "gate_t")}
        warmed = sem("warmed")
        out_done = sem("out_done")
        cleared = range(x_in.num, out_done.num + 1)

        def cols(h):
            return slice(h * HALF, (h + 1) * HALF)

        def two(ap):
            return ap.rearrange("p (a s) -> p a s", a=2)

        def pair(rows=P):
            return ps[0:rows, OB:SM + 1:SM - OB, :]

        def pair_bank(h):
            return (OB, SM)[h]

        with nc.Block() as block:
            @block.sync
            def _(sp):
                loads = ((wt[:, :, :], wts), (vec[:, :], vecs), (posw[:, :], pos), (sa1w[:, :], sa1),
                         (sa2w[:, :, :], sa2), (sa3w[:, :], sa3), (b1w[:, :, :], b1), (b2w[:, :], b2),
                         (gww[:, :], gw), (gbw[:, :, :], gb), (iow[:, :, :], iota))
                sp.dma_start(xin[:, :], x[0]).then_inc(x_in, 16)
                for dst, src in loads:
                    sp.dma_start(dst, src).then_inc(weights_in, 16)
                sp.wait_ge(weights_in, 16 * len(loads))

            @block.gpsimd
            def _(pool):
                pool.memset(ks[ROWS:ROWS + 3, 1:3, :, :], 1.0).then_inc(pool_set, 1)
                pool.wait_ge(pool_set, 1)
                pool.memset(va[1][:, :, :, :], 1.0).then_inc(pool_set, 1)
                pool.memset(oatt[:, :, :], 1.0).then_inc(pool_set, 1)
                pool.memset(tok[:, :, :], 0.0).then_inc(pool_set, 1)
                pool.wait_ge(pool_set, 4)

            @block.vector
            def _(dve):
                dve.memset(conv_in[:, :, :], 0.0).then_inc(consts_set, 1)
                dve.memset(low[:, :], 0.0).then_inc(consts_set, 1)
                dve.memset(ks[ROWS:ROWS + 3, 0:1, :, :], 1.0).then_inc(consts_set, 1)
                dve.memset(va[0][:, :, :, :], 1.0).then_inc(consts_set, 1)
                dve.memset(km[MD:MD + 1, :, :], 1.0).then_inc(consts_set, 1)
                dve.wait_ge(weights_in, 16 * 11)
                for i, name in enumerate(("ff_b1", "sa_b1", "sa_b2", "sa_b3")):
                    dve.tensor_scalar(half_b[:, i:i + 1], v(name), 0.5, None, ALU.mult).then_inc(consts_set, 1)
                dve.wait_ge(consts_set, 9)

        def sync_program(sp, img, conv, experts, token, front, small):
            def spread_parts(a, i):
                sp.wait_ge(done[f"{'kq'[i]}3_{'ab'[a]}"], 2 if a == 0 else 1)
                sp.dma_start(parts_dram[a, i], parts[:, i, :, :]).then_inc(parts_out[a][i], 16)

            def spread_group(a, i, g):
                sp.wait_ge(parts_out[a][i], 16)
                for run, count in enumerate(RUNS):
                    first = sum(RUNS[0:run])
                    for j in range(count):
                        dst = (ks, qs)[i][HD * (first + j):HD * (first + j + 1), slot_of(a, g), :, :]
                        src = parts_dram[a, i, GH * HD * g:GH * HD * (g + 1), (j, run)[i], :]
                        sp.dma_start(dst, src.rearrange("(h d) s -> d h s", d=HD)).then_inc(spread[a][g], 16)

            def spread_max(f, u):
                a, _, _, first = FAMILIES[f]
                n = (u - first) // 2 + 1
                sp.wait_ge(rows_split[f], n)
                if u < NH:
                    sp.dma_start(maxrow_dram[a, u // 2], maxrow[:, u // 2 % 2, :, :]).then_inc(rows_out[f], 16)
                    sp.wait_ge(rows_out[f], 16 * n)
                    dst = qs[ROWS:ROWS + 3, slot_of(a, u // GH), u % GH:u % GH + 2, :]
                    sp.dma_start(dst.rearrange("r h (t s) -> r (h t) s", t=NT),
                                 maxrow_dram[a, u // 2].rearrange("t r s -> r t s")).then_inc(rows_in[f], 16)
                else:
                    sp.dma_start(maxrow_m_dram, maxrow_m[:, :]).then_inc(rows_out[f], 16)
                    sp.wait_ge(rows_out[f], 16 * n)
                    sp.dma_start(qm[MD:MD + 1, :, :].rearrange("a m s -> a (m s)"),
                                 maxrow_m_dram.rearrange("(a t) s -> a (t s)", a=1)).then_inc(rows_in[f], 16)

            def fetch(e):
                if e == 0 and conv:
                    sp.wait_ge(blocks_used["a1"], 160 - A_FRONT)
                if e >= 2:
                    sp.wait_ge(y_ready, 2 * (e - 1))
                if e >= 1:
                    sp.wait_ge(weights_ready, 32 * e)
                sp.dma_start(w1e[e % 2], w1[:, e, :]).then_inc(weights_ready, 16)
                sp.dma_start(w2e[e % 2], w2[:, e, :]).then_inc(weights_ready, 16)

            if conv:
                for u in (4, 6, 8):
                    spread_max("a1", u)
            if experts:
                for e in range(3):
                    fetch(e)
            if token:
                sp.wait_ge(done["xr"], 1)
                sp.dma_start(xin[:, :], x[bass.ds((img + 1) % NB, 1)].rearrange("a p s -> (a p) s")
                             ).then_inc(x_in, 16)
                fetch(3)
                sp.wait_ge(pv_done[0], 2 * STEPS)
                spread_parts(1, 0)
                fetch(4)
                spread_group(1, 0, 0)
                spread_parts(1, 1)
                spread_group(1, 1, 0)
                fetch(5)
                for i in range(2):
                    spread_group(1, i, 1)
                fetch(6)
                spread_max("b", 0)
                fetch(7)
                spread_max("b", 2)
            elif experts:
                for e in range(3, NE):
                    fetch(e)
            if experts:
                sp.wait_ge(result, 2)
                last = (img - 1 + NB) % NB if token else NB - 1
                sp.dma_start(out[bass.ds(last, 1)].rearrange("a p s -> (a p) s"), xe[:, :]).then_inc(out_done, 16)
            if front:
                spread_parts(0, 0)
                spread_group(0, 0, 0)
                if token:
                    spread_max("b", 4)
                spread_parts(0, 1)
                spread_group(0, 1, 0)
                if token:
                    spread_max("b", 6)
                if token:
                    sp.wait_ge(pv_done[1], STEPS)
                for i in range(2):
                    spread_group(0, i, 1)
                spread_max("a0", 0)
                spread_max("a0", 2)
                sp.wait_ge(spread[0][0], 16 * 2 * PIECES)
                sp.wait_ge(spread[0][1], 16 * 2 * PIECES)
                sp.wait_ge(rows_in["a0"], 16 * 2)
            if experts:
                sp.wait_ge(out_done, 16)

        def pool_program(pool, conv, experts, token, front, small):
            def rstd(name, n):
                pool.wait_ge(done[name.replace("rstd", "var")], 1)
                pool.tensor_tensor(rs[:, 0:n], vn[:, 0:n], v("neg_half").to_broadcast([P, n]),
                                   ALU.pow).then_inc(done[name], 1)

            if experts:
                rstd("ln_rstd_e", NT)
            if token:
                rstd("post_rstd", 1)
                rstd("ln_rstd_b", NT)
            if front:
                rstd("pre_rstd", 1)
                rstd("norm_rstd", 1)
                for i, x in enumerate("kq"):
                    for h in range(2):
                        pool.wait_ge(done[f"{x}2_a"], h + 1)
                        pool.tensor_tensor(parts[:, i, 2, cols(h)], rem[:, cols(h)], parts[:, i, 1, cols(h)],
                                           ALU.subtract).then_inc(done[f"{x}3_a"], 1)
                for h in range(2):
                    pool.wait_ge(done["tanh1"], h + 1)
                    pool.wait_ge(small_free, small[f"c1{h}"])
                    for dx in range(3):
                        qd = slice(32 * dx, 32 * dx + 32)
                        lo, hi = max(0, 1 - dx), min(SIDE, SIDE + 1 - dx)

                        def shifted(ap):
                            return ap[qd, cols(h)].rearrange("p (y x) -> p y x", x=SIDE)[:, :, lo + dx - 1:hi + dx - 1]

                        dst = conv_in[qd, 1 + 16 * h:17 + 16 * h, lo:hi]
                        pool.tensor_tensor(dst, shifted(ta), shifted(tb), ALU.mult).then_inc(done["conv_in_dx"], 1)
                        pool.wait_ge(done["conv_in_dx"], 3 * h + dx + 1)
                        pool.tensor_tensor(dst, dst, shifted(tb), ALU.add).then_inc(done["conv_in"], 1)
                for h in range(2):
                    pool.wait_ge(small_free, small[f"c3{h}"])
                    pool.tensor_tensor(gated[:, cols(h)], ta[:, cols(h)], x1[:, cols(h)], ALU.mult
                                       ).then_inc(done["gated"], 1)
                    pool.wait_ge(done["gated"], 2 * h + 1)
                    pool.tensor_tensor(gated[:, cols(h)], gated[:, cols(h)], x1[:, cols(h)], ALU.add
                                       ).then_inc(done["gated"], 1)
                pool.wait_ge(done["gated"], 4)

        def tensor_program(pe, conv, experts, token, front, small):
            def start_small(name):
                if small[name] > 1:
                    pe.wait_ge(small_free, small[name] - 1)

            def max_block(f, j):
                a, first, _, _ = FAMILIES[f]
                u, t, k = block_of(j)
                n = j - first
                if n == 0:
                    if f == "a0":
                        pe.wait_ge(spread[0][0], 16 * 2 * PIECES)
                        if token:
                            pe.wait_ge(blocks_used["b"], 128)
                if (f, j) == ("a0", 64):
                    pe.wait_ge(spread[0][1], 16 * 2 * PIECES)
                if n == 0:
                    if f == "b":
                        pe.wait_ge(spread[1][0], 16 * 2 * PIECES)
                        pe.wait_ge(blocks_used["a1"], 160 - A_FRONT)
                if f == "b" and j == 64:
                    pe.wait_ge(spread[1][1], 16 * 2 * PIECES)
                if u >= NH and (t, k) == (0, 0):
                    pe.wait_ge(small_free, small[f"km{u - NH}1"])
                    pe.wait_ge(small_free, small[f"qm{u - NH}1"])
                if n >= 2:
                    pe.wait_ge(blocks_used[f], n - 1)
                if u < NH:
                    slot = slot_of(a, u // GH)
                    lhs, rhs = qs[0:ROWS, slot, u % GH, t * P:(t + 1) * P], ks[0:ROWS, slot, u % GH, cols(k)]
                else:
                    lhs, rhs = qmh[:, u - NH, t * P:(t + 1) * P], kmh[:, u - NH, cols(k)]
                pe.matmul(ps[:, MX + n % 2, :], lhs, rhs, start=True, stop=True).then_inc(blocks_ready[f], 1)

            def transposes(bank, src, count=4, rows=P):
                for t in range(count):
                    mm = pe.transpose(ps[0:rows, bank, t * P:(t + 1) * P], src(t), w("ident"))
                return mm

            def half_product(weight, src, h, m=P):
                return pe.matmul(ps[0:m, SM, :], weight, src[:, cols(h)], start=True, stop=True)

            def pair_product(weight, src):
                for h in range(2):
                    mm = pe.matmul(ps[:, pair_bank(h), :], weight, src[:, cols(h)], start=True, stop=True)
                return mm

            def small_product(name):
                start_small(name)
                if name.startswith("turn"):
                    _, f, u = name.split("_")
                    u = int(u)
                    pe.wait_ge(max_ready[f], u - FAMILIES[f][3] + 2)
                    mm = pe.transpose(ps[0:2 * NT, SM, 0:P], negmax[:, u:u + 2, :].rearrange("p u t -> p (u t)"),
                                      w("ident"))
                elif name.startswith("tra"):
                    f = int(name[3:])
                    pe.wait_ge(o_taken[0], f + 1)
                    mm = transposes(SM, lambda t: oatt[:, f, t * P:(t + 1) * P])
                elif name.startswith("tob"):
                    q = int(name[3:])
                    mm = transposes(SM, lambda t: tok[:, 4 * q + t, :])
                elif name.startswith("mtr"):
                    q = int(name[3:])
                    pe.wait_ge(mo_taken, q + 1)
                    for t in range(4):
                        pe.transpose(ps[:, MX + q, t * MD:(t + 1) * MD], tb[0:MD, HALF + t * P:HALF + (t + 1) * P],
                                     w("ident")[0:MD, 0:MD])
                    mm = transposes(SM, lambda t: tb[:, t * P:(t + 1) * P])
                elif name.startswith("mtb"):
                    q = int(name[3:])
                    mm = transposes(SM, lambda t: ta[:, (4 * q + t) * P:(4 * q + t + 1) * P])
                elif name in ("pre", "norm", "post"):
                    pe.wait_ge(done[f"{name}_stats"], 1)
                    mm = pe.matmul(ps[:, SM, 0:2], w("group"), mv[:, 0, :], start=True, stop=True)
                elif name in ("kA0", "kA1", "qA0", "qA1"):
                    pe.wait_ge(done["xh_a"], 1)
                    mm = half_product(w("w" + name[0]), xh, int(name[2]))
                elif name in ("vA0", "vA1", "vm0", "vm1"):
                    h = int(name[2])
                    for t in range(4):
                        tt = 4 * h + t
                        mm = pe.matmul(ps[:, SM, t * P:(t + 1) * P], xh[:, tt * P:(tt + 1) * P],
                                       w("wv" if name[1] == "A" else "wvm"), start=True, stop=True)
                elif name in ("c10", "c11"):
                    pe.wait_ge(done["x1"], 1)
                    mm = half_product(sa1w[:, :], x1, int(name[2]), 96)
                elif name in ("c20", "c21"):
                    h = int(name[2])
                    pe.wait_ge(done["conv_in"], 6)
                    for dy in range(3):
                        mm = pe.matmul(ps[0:HD, SM, :], sa2w[:, dy, :],
                                       conv_in[:, 16 * h + dy:16 * h + dy + 16, :].rearrange("p y x -> p (y x)"),
                                       start=(dy == 0), stop=(dy == 2))
                elif name in ("c30", "c31"):
                    pe.wait_ge(done["conv2"], 1 + int(name[2]))
                    mm = half_product(sa3w[:, :], conv2, int(name[2]))
                elif name.startswith("km"):
                    mm = half_product(w(f"wkm{name[2]}"), xh, int(name[3]))
                elif name.startswith("qm"):
                    mm = half_product(w(f"wqm{name[2]}"), gated, int(name[3]))
                elif name.startswith("tro"):
                    f = int(name[3:])
                    mm = transposes(SM, lambda t: oatt[:, f, t * P:(t + 1) * P])
                elif name.startswith("trn"):
                    h = int(name[3:])
                    pe.wait_ge(done["ln_e"], 1)
                    mm = transposes(SM, lambda t: lnt[:, 4 * h + t, :])
                elif name == "logits":
                    pe.wait_ge(done["xe"], 2)
                    for t in range(NT):
                        mm = pe.matmul(ps[:, SM, t * NE:(t + 1) * NE], xe[:, t * P:(t + 1) * P], gww[:, :],
                                       start=True, stop=True)
                elif name.startswith("trg"):
                    h = int(name[3:])
                    pe.wait_ge(done["gates"], 1)
                    mm = transposes(SM, lambda t: gate[:, 4 * h + t, :], rows=NE)
                elif name.startswith("b2"):
                    h = int(name[2:])
                    pe.wait_ge(done["gate_t"], 1 + h)
                    for t in range(4):
                        tt = 4 * h + t
                        mm = pe.matmul(ps[:, SM, t * P:(t + 1) * P], low[:, tt * P:(tt + 1) * P], b2w[:, :],
                                       start=True, stop=True)
                elif name == "ff1":
                    for q in range(2):
                        bank = ps[:, pair_bank(q), :]
                        pe.matmul(bank, w("ffa"), oatt[:, q, :], start=True, stop=False)
                        mm = pe.matmul(bank, w("ffb"), omul[:, cols(q)], start=False, stop=True)
                elif name == "ff2":
                    pe.wait_ge(done["ff_act"], 1)
                    mm = pair_product(w("ff2"), tb)
                elif name == "outp":
                    pe.wait_ge(done["ff2"], 1)
                    mm = pair_product(w("out"), ta)
                elif name == "tr_x":
                    pe.wait_ge(done["xr"], 1)
                    for h in range(2):
                        mm = transposes(pair_bank(h), lambda t: x1[:, (4 * h + t) * P:(4 * h + t + 1) * P])
                elif name == "tr_nb":
                    pe.wait_ge(done["ln_b"], 1)
                    for h in range(2):
                        mm = transposes(pair_bank(h), lambda t: lnt[:, 4 * h + t, :])
                elif name in ("kB", "qB"):
                    pe.wait_ge(done["xh_b"], 1)
                    mm = pair_product(w(f"w{name}"), xh)
                elif name == "vB":
                    for t in range(NT):
                        mm = pe.matmul(ps[:, pair_bank(t // 4), (t % 4) * P:(t % 4 + 1) * P], xh[:, t * P:(t + 1) * P],
                                       w("wvB"), start=True, stop=True)
                mm.then_inc(small_full, 1)

            def scores(a, n, pr):
                g, q, t = n // STEPS, n // NT % 2, n % NT
                if n % STEPS == 0 and pr == 0 and (a, g) != (0, 0):
                    f = "a1" if a == 0 else "b"
                    pe.wait_ge(rows_in[f], 16 * 2 * (1 if a == 0 else g + 1))
                if n >= 1:
                    pe.wait_ge(exp_done[a], 2 * (n - 1) + pr + 1)
                elif a == 1:
                    pe.wait_ge(y_used, UNITS)
                    pe.wait_ge(result, 2)
                for j in range(2):
                    h = 2 * pr + j
                    mm = pe.matmul(ps[:, SC + h, :], ks[:, slot_of(a, g), h, t * P:(t + 1) * P],
                                   qs[:, slot_of(a, g), h, cols(q)], start=True, stop=True)
                mm.then_inc(scores_ready[a], 1)

            def weigh_values(a, n):
                g, t = n // STEPS, n % NT
                pe.wait_ge(exp_done[a], 2 * n + 2)
                if t == 0 and n:
                    pe.wait_ge(o_taken[a], n // NT)
                if a == 1 and n == 0:
                    pe.wait_ge(done["v_b"], 1)
                for j in range(GH):
                    mm = pe.matmul(ps[32 * j:32 * j + 32, OB, :], va[a][:, t, GH * g + j, :], prob[:, n % 3, j, :],
                                   start=(t == 0), stop=(t == NT - 1))
                mm.then_inc(pv_done[a], 1)

            def attention_step(a, n, blocks, run):
                for f, j in blocks[0:1]:
                    max_block(f, j)
                if run:
                    scores(a, n, 0)
                for f, j in blocks[1:2]:
                    max_block(f, j)
                if run:
                    scores(a, n, 1)
                for f, j in blocks[2:3]:
                    max_block(f, j)
                if run and n:
                    weigh_values(a, n - 1)
                for f, j in blocks[3:]:
                    max_block(f, j)

            if experts:
                for n in range(2 * STEPS):
                    attention_step(0, n, conv_blocks(n) if conv else [], conv)
                    for name in CONV_WINDOW.get(n, ()):
                        if conv or for_last_norm(name):
                            small_product(name)

            if conv:
                pe.wait_ge(rows_in["a1"], 16 * 3)
                for n in range(STEPS + 1):
                    if n < STEPS:
                        q, t = n // NT, n % NT
                        if n >= 2:
                            pe.wait_ge(mexp_done, n - 1)
                        else:
                            pe.wait_ge(exp_done[0], 4 * STEPS)
                        for m in range(MULTI):
                            mm = pe.matmul(ps[:, SC + 2 * (n % 2) + m, :], km[:, m, t * P:(t + 1) * P],
                                           qm[:, m, cols(q)], start=True, stop=True)
                        mm.then_inc(ms_ready, 1)
                    if n == 0:
                        weigh_values(0, 2 * STEPS - 1)
                    if n >= 1:
                        q, t = (n - 1) // NT, (n - 1) % NT
                        if n == 1:
                            pe.wait_ge(o_taken[0], 4)
                            pe.wait_ge(blocks_used["a1"], 160 - A_FRONT)
                        if n == NT + 1:
                            pe.wait_ge(mo_taken, 1)
                        pe.wait_ge(mexp_done, n)
                        for m in range(MULTI):
                            pe.matmul(ps[MD * m:MD * (m + 1), OB, :], vm[:, t, MD * m:MD * (m + 1)],
                                      prob[:, (n - 1) % 3, m, :], start=(t == 0), stop=(t == NT - 1))
                        for m in range(MULTI):
                            mm = pe.matmul(ps[32 * m:32 * (m + 1), MX + q, :], w("ones")[:, 0:32],
                                           prob[:, (n - 1) % 3, m, :], start=(t == 0), stop=(t == NT - 1))
                        mm.then_inc(mpv_done, 1)
                    for name in PARTS_WINDOW.get(n, ()):
                        small_product(name)

            def hidden(u, blocks):
                e, h = u // 2, u % 2
                if h == 0:
                    pe.wait_ge(weights_ready, 32 * (e + 1))
                for c in range(NC):
                    n = NC * u + c
                    if n >= 2:
                        pe.wait_ge(gelu_done, n - 1)
                    elif conv:
                        pe.wait_ge(mexp_done, STEPS)
                    pe.matmul(ps[:, SC + n % 2, :], w1e[e % 2][:, c * P:(c + 1) * P], xe[:, cols(h)],
                              start=True, stop=True).then_inc(hid_ready, 1)
                    for f, j in blocks[c:c + 1] if c < NC - 1 else blocks[c:]:
                        max_block(f, j)

            def expert_out(u, blocks):
                e = u // 2
                pe.wait_ge(gelu_done, NC * (u + 1))
                if u >= 2:
                    pe.wait_ge(y_used, u - 1)
                for t in range(4):
                    for c in range(NC):
                        mm = pe.matmul(ps[:, SC + 2 + u % 2, t * P:(t + 1) * P], prob[:, u % 2, c, t * P:(t + 1) * P],
                                       w2e[e % 2][:, c * P:(c + 1) * P], start=(c == 0), stop=(c == NC - 1))
                    if t == 3:
                        mm.then_inc(y_ready, 1)
                    for f, j in blocks[t:t + 1] if t < 3 else blocks[t:]:
                        max_block(f, j)

            if experts:
                for s in range(SLOTS):
                    blocks = expert_blocks(s) if token else []
                    if s % 2 == 0 and s // 2 < UNITS:
                        hidden(s // 2, blocks)
                    elif s % 2 == 1 and s >= 3:
                        expert_out((s - 3) // 2, blocks)
                    else:
                        for f, j in blocks:
                            max_block(f, j)
                    if token:
                        for name in EXPERT_WINDOW.get(s, ()):
                            if name == "ff1":
                                pe.wait_ge(mo_taken, 2)
                            small_product(name)
                pe.wait_ge(y_used, UNITS)
                for h in range(2):
                    transposes(SC + h, lambda t: toke[:, 4 * h + t, :]).then_inc(result_ready, 1)

            if front and not token:
                small_product("pre")
                small_product("norm")
            if front:
                for n in range(2 * STEPS):
                    attention_step(1, n, token_blocks(n, token), token)
                    for name in TOKEN_WINDOW.get(n, ()):
                        if token or for_front(name):
                            small_product(name)
                if token:
                    weigh_values(1, 2 * STEPS - 1)

        def scalar_program(act, conv, experts, token, front, small):
            def half(dst, src, bias):
                act.activation(dst, src, ACT.Identity, bias=bias, scale=0.5).then_inc(small_free, 1)

            def read_small(dst, src, name, event, func=ACT.Copy, free=False, **kw):
                act.wait_ge(small_full, small[name])
                ins = act.activation(dst, src, func, **kw)
                if free or event:
                    ins.then_inc(small_free if free else done[event], 1)

            def small_product(name):
                if name in ("kA0", "kA1", "qA0", "qA1"):
                    i, h = "kq".index(name[0]), int(name[2])
                    read_small(parts[:, i, 0, cols(h)], ps[:, SM, :], name, f"{name[0]}1_a")
                elif name in ("c10", "c11"):
                    act.wait_ge(done["q3_a"], int(name[2]) + 1)
                    read_small(ta[0:96, cols(int(name[2]))], ps[0:96, SM, :], name, "tanh1", ACT.Tanh,
                               bias=half_b[0:96, 1:2], scale=0.5)
                    half(tb[0:96, cols(int(name[2]))], ps[0:96, SM, :], half_b[0:96, 1:2])
                elif name in ("c20", "c21"):
                    read_small(ta[0:HD, cols(int(name[2]))], ps[0:HD, SM, :], name, "tanh2", ACT.Tanh,
                               bias=half_b[0:HD, 2:3], scale=0.5)
                    half(tb[0:HD, cols(int(name[2]))], ps[0:HD, SM, :], half_b[0:HD, 2:3])
                elif name in ("c30", "c31"):
                    read_small(ta[:, cols(int(name[2]))], ps[:, SM, :], name, "", ACT.Tanh, free=True,
                               bias=half_b[:, 3:4], scale=0.5)
                elif name in ("vA0", "vA1"):
                    h = int(name[2])
                    read_small(va[0][:, 4 * h:4 * h + 4, :, 0:HD],
                               ps[:, SM, :].rearrange("p (t h d) -> p t h d", t=4, h=NH), name, "", free=True)
                elif name in ("vm0", "vm1"):
                    h = int(name[2])
                    read_small(vm[:, 4 * h:4 * h + 4, :].rearrange("p t c -> p (t c)"), ps[:, SM, :], name, "", free=True)
                elif name.startswith("km"):
                    m, h = int(name[2]), int(name[3])
                    read_small(km[0:MD, m, cols(h)], ps[0:MD, SM, :], name, "")
                    act.activation(kmh[:, m, cols(h)], ps[:, SM, :], ACT.Copy).then_inc(small_free, 1)
                elif name.startswith("qm"):
                    m, h = int(name[2]), int(name[3])
                    read_small(qm[0:MD, m, cols(h)], ps[0:MD, SM, :], name, "", scale=0.5)
                    act.activation(qmh[:, m, cols(h)], ps[:, SM, :], ACT.Copy, scale=0.5).then_inc(done["qmh"], 1)
                elif name.startswith("tob"):
                    read_small(oatt[:, int(name[3:]), :], ps[:, SM, :], name, "", free=True)
                elif name.startswith("mtb"):
                    read_small(omul[:, cols(int(name[3:]))], ps[:, SM, :], name, "", free=True)
                elif name.startswith("trn"):
                    read_small(xe[:, cols(int(name[3:]))], ps[:, SM, :], name, "xe")
                elif name == "ff1":
                    read_small(two(ta[:, :]), pair(), name, "tanh_ff", ACT.Tanh, bias=half_b[:, 0:1], scale=0.5)
                elif name == "ff2":
                    read_small(two(ta[:, :]), pair(), name, "ff2", ACT.Identity, bias=v("ff_b2"))
                elif name == "outp":
                    read_small(two(tb[:, :]), pair(), name, "outp", ACT.Identity, bias=v("out_b"))
                elif name == "tr_x":
                    read_small(tok[:, :, :].rearrange("p (a t) c -> p a (t c)", a=2), pair(), name, "tok")
                elif name == "tr_nb":
                    read_small(two(xh[:, :]), pair(), name, "xh_b")
                elif name in ("kB", "qB"):
                    i = "kq".index(name[0])
                    read_small(two(parts[:, i, 0, :]), pair(), name, f"{name[0]}1_b")

            def second_part_b(name):
                i = "kq".index(name[0])
                act.wait_ge(done[f"{name[0]}_rem_b"], 1)
                act.activation(parts[:, i, 1, :], rem[:, :], ACT.Copy).then_inc(done[f"{name[0]}2_b"], 1)

            def second_part(name):
                i, h = "kq".index(name[0]), int(name[2])
                act.wait_ge(done[f"{name[0]}_rem_a"], h + 1)
                act.activation(parts[:, i, 1, cols(h)], rem[:, cols(h)], ACT.Copy).then_inc(done[f"{name[0]}2_a"], 1)

            def take_output(a, f):
                act.wait_ge(pv_done[a], NT * (f + 1))
                act.activation(oatt[:, f, :], ps[:, OB, :], ACT.Copy).then_inc(o_taken[a], 1)

            def exps(a, n):
                if n >= 3:
                    act.wait_ge(pv_done[a], n - 2)
                for pr in range(2):
                    act.wait_ge(scores_ready[a], 2 * n + pr + 1)
                    act.activation(prob[:, n % 3, 2 * pr:2 * pr + 2, :], ps[:, SC + 2 * pr:SC + 2 * pr + 2, :], ACT.Exp,
                                   scale=HD ** -0.5).then_inc(exp_done[a], 1)
                if n and n % NT == 0:
                    take_output(a, n // NT - 1)

            if experts:
                for n in range(2 * STEPS):
                    if conv:
                        exps(0, n)
                    for name in CONV_WINDOW.get(n, ()):
                        if conv or for_last_norm(name):
                            small_product(name)
                    if n == 25:
                        act.wait_ge(done["gate_diff"], 1)
                        act.activation(ex[:, :, :], logit[:, :, :], ACT.Exp).then_inc(done["gate_exp"], 1)
            if conv:
                take_output(0, 3)
                for n in range(STEPS):
                    if n >= 3:
                        act.wait_ge(mpv_done, n - 2)
                    act.wait_ge(ms_ready, n + 1)
                    act.activation(prob[:, n % 3, 0:2, :], ps[:, SC + 2 * (n % 2):SC + 2 * (n % 2) + 2, :], ACT.Exp,
                                   scale=MD ** -0.5).then_inc(mexp_done, 1)
                    for name in PARTS_WINDOW.get(n, ()):
                        small_product(name)
                act.activation(warm[:, :], half_b[:, 0:1], ACT.Gelu).then_inc(warmed, 1)
                act.wait_ge(mpv_done, STEPS)
            if experts:
                for s in range(SLOTS):
                    u = s // 2
                    if s % 2 == 0 and u < UNITS:
                        if u >= 2:
                            act.wait_ge(y_ready, u - 1)
                        for c in range(NC):
                            n = NC * u + c
                            act.wait_ge(hid_ready, n + 1)
                            act.activation(prob[:, u % 2, c, :], ps[:, SC + n % 2, :], ACT.Gelu,
                                           bias=b1w[:, u // 2, c:c + 1]).then_inc(gelu_done, 1)
                    if token:
                        for name in EXPERT_WINDOW.get(s - 1, ()):
                            if name in ("kB", "qB"):
                                second_part_b(name)
                        for name in EXPERT_WINDOW.get(s, ()):
                            small_product(name)
                for h in range(2):
                    act.wait_ge(result_ready, h + 1)
                    act.activation(xe[:, cols(h)], ps[:, SC + h, :], ACT.Copy).then_inc(result, 1)
            if front:
                for n in range(2 * STEPS):
                    if token:
                        if n == 0:
                            act.wait_ge(y_ready, UNITS)
                        exps(1, n)
                    for name in TOKEN_WINDOW.get(n - 2, ()):
                        if name in ("kA0", "kA1", "qA0", "qA1"):
                            second_part(name)
                    for name in TOKEN_WINDOW.get(n, ()):
                        if token or for_front(name):
                            small_product(name)
                if token:
                    take_output(1, 3)

        def vector_program(dve, conv, experts, token, front, small):
            chain = [0]
            blocks_left = []

            def note(ins):
                chain[0] += 1
                ins.then_inc(dve_chain, 1)

            def sync():
                dve.wait_ge(dve_chain, chain[0])

            def reduce_next():
                if blocks_left:
                    reduce_block(*blocks_left.pop(0))

            def link(ins):
                note(ins)
                reduce_next()
                sync()

            def read_small(name):
                dve.wait_ge(small_full, small[name])

            def freed(name):
                reduce_next()
                dve.wait_ge(small_free, small[name])

            def group_stats(src, name):
                for h in range(2):
                    note(dve.bn_stats(st[:, h, :], src[:, cols(h)]))
                sync()
                link(dve.bn_aggr(mv[:, 0, :], st[:, 0:2, :]))
                dve.scalar_tensor_tensor(out=mv[:, 0, 1:2], in0=mv[:, 0, 0:1], scalar=mv[:, 0, 0:1],
                                         in1=mv[:, 0, 1:2], op0=ALU.mult, op1=ALU.add).then_inc(done[f"{name}_stats"], 1)

            def group_var(name):
                read_small(name)
                dve.tensor_copy(gs[:, :], ps[:, SM, 0:2]).then_inc(small_free, 1)
                freed(name)
                link(dve.tensor_tensor(nb[:, 0:1], gs[:, 0:1], gs[:, 0:1], ALU.mult))
                link(dve.scalar_tensor_tensor(out=vn[:, 0:1], in0=nb[:, 0:1], scalar=-1.0, in1=gs[:, 1:2],
                                              op0=ALU.mult, op1=ALU.add))
                dve.tensor_scalar(vn[:, 0:1], vn[:, 0:1], 0.0, EPS_GN, ALU.max, ALU.add).then_inc(done[f"{name}_var"], 1)

            def group_coefs(name):
                dve.wait_ge(done[f"{name}_rstd"], 1)
                link(dve.tensor_tensor(ca[:, :], rs[:, 0:1], v(f"{name}_g"), ALU.mult))
                link(dve.tensor_tensor(nb[:, 0:1], gs[:, 0:1], ca[:, :], ALU.mult))
                link(dve.tensor_tensor(cb[:, :], v(f"{name}_b"), nb[:, 0:1], ALU.subtract))

            def layer_stats(src, name):
                for t in range(NT):
                    note(dve.bn_stats(st[:, t, :], src[:, t, :]))
                    if t % 3 == 2:
                        reduce_next()
                sync()
                for t in range(NT):
                    note(dve.bn_aggr(mv[:, t, :], st[:, t, :]))
                sync()
                dve.tensor_scalar(vn[:, :], mv[:, :, 1], 0.0, EPS_LN, ALU.max, ALU.add
                                  ).then_inc(done[f"ln_var_{name}"], 1)

            def layer_norm(src, name):
                dve.wait_ge(done[f"ln_rstd_{name}"], 1)
                link(dve.scalar_tensor_tensor(out=nb[:, :], in0=mv[:, :, 0], scalar=-1.0, in1=rs[:, :],
                                              op0=ALU.mult, op1=ALU.mult))
                for t in range(NT):
                    ins = dve.tensor_scalar(lnt[:, t, :], src[:, t, :], rs[:, t:t + 1], nb[:, t:t + 1],
                                            ALU.mult, ALU.add)
                    if t < NT - 1:
                        note(ins)
                        if t % 3 == 2:
                            reduce_next()
                ins.then_inc(done[f"ln_{name}"], 1)

            def reduce_block(f, j):
                a, first, _, _ = FAMILIES[f]
                u, t, k = block_of(j)
                n = j - first
                dve.wait_ge(blocks_ready[f], n + 1)
                dve.tensor_reduce(blockmax[:, u, t, k:k + 1], ps[:, MX + n % 2, :], AX.X, ALU.max
                                  ).then_inc(blocks_used[f], 1)
                if j % 16 == 15:
                    dve.wait_ge(blocks_used[f], n + 1)
                    dve.tensor_reduce(negmax[:, u, :], blockmax[:, u, :, :], AX.X, ALU.max, negate=True
                                      ).then_inc(max_ready[f], 1)

            def split_max(name):
                _, f, u = name.split("_")
                u = int(u)
                n = (u - FAMILIES[f][3]) // 2 + 1
                read_small(name)
                src = ps[0:2 * NT, SM, 0:P]
                if u >= NH:
                    dve.tensor_copy(maxrow_m[:, :], src).then_inc(small_free, 1)
                    freed(name)
                    dve.sem_inc(rows_split[f], 1)
                    return
                if n >= 3:
                    dve.wait_ge(rows_out[f], 16 * (n - 2))
                row = maxrow[:, u // 2 % 2, :, :]
                link(dve.tensor_copy(row[:, 0, :], src))
                dve.tensor_tensor(rowrem[:, :], src, row[:, 0, :], ALU.subtract).then_inc(small_free, 1)
                freed(name)
                link(dve.tensor_copy(row[:, 1, :], rowrem[:, :]))
                dve.tensor_tensor(row[:, 2, :], rowrem[:, :], row[:, 1, :], ALU.subtract).then_inc(rows_split[f], 1)
                reduce_next()
                dve.wait_ge(rows_split[f], n)

            def third_part_b(name):
                i = "kq".index(name[0])
                dve.wait_ge(done[f"{name[0]}2_b"], 1)
                dve.tensor_tensor(parts[:, i, 2, :], rem[:, :], parts[:, i, 1, :], ALU.subtract
                                  ).then_inc(done[f"{name[0]}3_b"], 1)

            def small_product(name):
                h = int(name[-1]) if name[-1].isdigit() else 0
                if name.startswith("turn"):
                    split_max(name)
                elif name == "stats_e":
                    layer_stats(toke, "e")
                elif name == "norm_e":
                    layer_norm(toke, "e")
                elif name == "gates":
                    gates()
                elif name.startswith("tra"):
                    g, q = h // 2, h % 2
                    read_small(name)
                    o = ps[:, SM, :].rearrange("p (t j r) -> p t j r", t=4, r=2 * HD)
                    link(dve.reciprocal(orec[:, :, :], o[:, :, :, HD]))
                    oview = tok[:, 4 * q:4 * q + 4, GH * HD * g:GH * HD * (g + 1)].rearrange("p t (j d) -> p t j d", d=HD)
                    dve.tensor_tensor(oview, o[:, :, :, 0:HD], orec[:, :, :].unsqueeze(3).to_broadcast([P, 4, GH, HD]),
                                      ALU.mult).then_inc(small_free, 1)
                    freed(name)
                elif name.startswith("mtr"):
                    read_small(name)
                    sums = ps[:, MX + h, 0:4 * MD].rearrange("p (t m r) -> p t m r", t=4, m=MULTI)
                    link(dve.reciprocal(orec[:, :, 0:MULTI], sums[:, :, :, 0]))
                    dve.tensor_tensor(ta[:, cols(h)].rearrange("p (t m d) -> p t m d", t=4, m=MULTI),
                                      ps[:, SM, :].rearrange("p (t m d) -> p t m d", t=4, m=MULTI),
                                      orec[:, :, 0:MULTI].unsqueeze(3).to_broadcast([P, 4, MULTI, MD]),
                                      ALU.mult).then_inc(small_free, 1)
                    freed(name)
                elif name in ("pre", "norm"):
                    group_var(name)
                elif name in ("kA0", "kA1", "qA0", "qA1"):
                    i = "kq".index(name[0])
                    dve.wait_ge(done[f"{name[0]}1_a"], h + 1)
                    if i == 1:
                        dve.wait_ge(done["k3_a"], h + 1)
                    dve.tensor_tensor(rem[:, cols(h)], ps[:, SM, :], parts[:, i, 0, cols(h)], ALU.subtract
                                      ).then_inc(small_free, 1)
                    freed(name)
                    dve.sem_inc(done[f"{name[0]}_rem_a"], 1)
                elif name in ("c20", "c21"):
                    dve.wait_ge(done["tanh2"], h + 1)
                    dve.wait_ge(small_free, small[name])
                    dve.scalar_tensor_tensor(out=conv2[0:HD, cols(h)], in0=ta[0:HD, cols(h)], scalar=1.0,
                                             in1=tb[0:HD, cols(h)], op0=ALU.add, op1=ALU.mult
                                             ).then_inc(done["conv2"], 1)
                elif name.startswith("qm"):
                    m = int(name[2])
                    dve.wait_ge(done["qmh"], 2 * m + h + 1)
                    dve.scalar_tensor_tensor(out=qmh[MD:P, m, cols(h)], in0=ps[MD:P, SM, :], scalar=0.5,
                                             in1=qmh[MD:P, m, cols(h)], op0=ALU.mult, op1=ALU.subtract
                                             ).then_inc(small_free, 1)
                elif name.startswith("tro"):
                    g, q = h // 2, h % 2
                    read_small(name)
                    o = ps[:, SM, :].rearrange("p (t j r) -> p t j r", t=4, r=2 * HD)
                    link(dve.reciprocal(orec[:, :, :], o[:, :, :, HD]))
                    oview = rec[:, 0:4 * GH * HD].rearrange("p (t j d) -> p t j d", t=4, d=HD)
                    dve.tensor_tensor(oview, o[:, :, :, 0:HD], orec[:, :, :].unsqueeze(3).to_broadcast([P, 4, GH, HD]),
                                      ALU.mult).then_inc(small_free, 1)
                    freed(name)
                    c = slice(GH * HD * g, GH * HD * (g + 1))
                    link(dve.tensor_tensor(toke[:, 4 * q:4 * q + 4, c], tok[:, 4 * q:4 * q + 4, c],
                                           rec[:, 0:4 * GH * HD].rearrange("p (t c) -> p t c", t=4), ALU.add))
                elif name == "logits":
                    read_small(name)
                    dve.tensor_tensor(logit[:, :, :], ps[:, SM, 0:NT * NE].rearrange("p (t e) -> p t e", t=NT),
                                      gbw[:, :, :], ALU.add).then_inc(small_free, 1)
                    freed(name)
                    for t in range(NT):
                        note(dve.max(top[:, t, :], logit[:, t, :]))
                    sync()
                    for t in range(NT):
                        note(dve.max_index(topi[:, t, :], top[:, t, :], logit[:, t, :]))
                    sync()
                    link(dve.tensor_copy(topf[:, :, :], topi[:, :, 0:2]))
                    dve.tensor_tensor(logit[:, :, :], logit[:, :, :], top[:, :, 0:1].to_broadcast([P, NT, NE]),
                                      ALU.subtract).then_inc(done["gate_diff"], 1)
                elif name.startswith("trg"):
                    read_small(name)
                    dve.tensor_copy(gate_t[:, cols(h)], ps[0:NE, SM, :]).then_inc(small_free, 1)
                    freed(name)
                    dve.sem_inc(done["gate_t"], 1)
                elif name.startswith("b2"):
                    read_small(name)
                    tv = toke[:, 4 * h:4 * h + 4, :].rearrange("p t c -> p (t c)")
                    dve.tensor_tensor(tv, tv, ps[:, SM, :], ALU.add).then_inc(small_free, 1)
                    freed(name)
                elif name == "ff1":
                    dve.wait_ge(done["tanh_ff"], 1)
                    dve.tensor_scalar(two(tb[:, :]), pair(), v("ff_b1"), 0.5, ALU.add, ALU.mult).then_inc(small_free, 1)
                    freed(name)
                    dve.scalar_tensor_tensor(out=tb[:, :], in0=ta[:, :], scalar=1.0, in1=tb[:, :],
                                             op0=ALU.add, op1=ALU.mult).then_inc(done["ff_act"], 1)
                elif name == "outp":
                    dve.wait_ge(done["outp"], 1)
                    dve.sem_inc(small_free, 1)
                    group_stats(tb, "post")
                elif name == "post":
                    group_var("post")
                    group_coefs("post")
                    link(dve.scalar_tensor_tensor(out=x1[:, :], in0=tb[:, :], scalar=ca[:, :], in1=xin[:, :],
                                                  op0=ALU.mult, op1=ALU.add))
                    dve.tensor_scalar(x1[:, :], x1[:, :], cb[:, :], None, ALU.add).then_inc(done["xr"], 1)
                elif name == "tr_x":
                    dve.wait_ge(done["tok"], 1)
                    dve.sem_inc(small_free, 1)
                    layer_stats(tok, "b")
                    layer_norm(tok, "b")
                elif name in ("ff2", "tr_nb"):
                    dve.wait_ge(done[{"ff2": "ff2", "tr_nb": "xh_b"}[name]], 1)
                    dve.sem_inc(small_free, 1)
                elif name.startswith("trn"):
                    dve.wait_ge(done["xe"], h + 1)
                    dve.sem_inc(small_free, 1)
                elif name in ("kB", "qB"):
                    i = "kq".index(name[0])
                    dve.wait_ge(done[f"{name[0]}1_b"], 1)
                    if i == 1:
                        dve.wait_ge(done["k3_b"], 1)
                    dve.tensor_tensor(two(rem[:, :]), pair(), two(parts[:, i, 0, :]), ALU.subtract).then_inc(small_free, 1)
                    freed(name)
                    dve.sem_inc(done[f"{name[0]}_rem_b"], 1)
                elif name == "vB":
                    read_small(name)
                    for hh in range(2):
                        ins = dve.tensor_copy(va[1][:, 4 * hh:4 * hh + 4, :, 0:HD],
                                              ps[:, pair_bank(hh), :].rearrange("p (t h d) -> p t h d", t=4, h=NH))
                        if hh == 0:
                            note(ins)
                    ins.then_inc(small_free, 1)
                    freed(name)
                    dve.sem_inc(done["v_b"], 1)

            def gates():
                link(dve.tensor_tensor(oh[:, :, :], iow[:, :, :], topf[:, :, 0:1].to_broadcast([P, NT, NE]),
                                       ALU.is_equal))
                link(dve.tensor_tensor(gate[:, :, :], iow[:, :, :], topf[:, :, 1:2].to_broadcast([P, NT, NE]),
                                       ALU.is_equal))
                link(dve.tensor_tensor(gate[:, :, :], gate[:, :, :], oh[:, :, :], ALU.add))
                dve.wait_ge(done["gate_exp"], 1)
                link(dve.tensor_reduce(esum[:, :], ex[:, :, :], AX.X, ALU.add))
                link(dve.reciprocal(erec[:, :], esum[:, :]))
                link(dve.tensor_tensor(gate[:, :, :], gate[:, :, :], ex[:, :, :], ALU.mult))
                dve.tensor_tensor(gate[:, :, :], gate[:, :, :], erec[:, :].unsqueeze(2).to_broadcast([P, NT, NE]),
                                  ALU.mult).then_inc(done["gates"], 1)
                dve.wait_ge(done["gates"], 1)

            def start_pre():
                dve.wait_ge(x_in, 16)
                group_stats(xin, "pre")

            def start_x1():
                group_coefs("pre")
                link(dve.scalar_tensor_tensor(out=x1[:, :], in0=xin[:, :], scalar=ca[:, :], in1=posw[:, :],
                                              op0=ALU.mult, op1=ALU.add))
                dve.tensor_scalar(x1[:, :], x1[:, :], cb[:, :], None, ALU.add).then_inc(done["x1"], 1)
                dve.wait_ge(done["x1"], 1)

            def start_xh():
                group_coefs("norm")
                dve.tensor_scalar(xh[:, :], x1[:, :], ca[:, :], cb[:, :], ALU.mult, ALU.add
                                  ).then_inc(done["xh_a"], 1)

            def attention_step(blocks, names, now):
                blocks_left.extend(blocks)
                reduce_next()
                for name in names:
                    small_product(name)
                while blocks_left:
                    reduce_next()
                for name in now:
                    small_product(name)

            if experts:
                late = []
                for n in range(2 * STEPS):
                    names = [x for x in CONV_WINDOW.get(n, ()) if conv or for_last_norm(x)]
                    attention_step(conv_blocks(n) if conv else [], late + CONV_EXTRA.get(n, []), names[:-1])
                    late = names[-1:]
            if conv:
                small_product("tra3")
                for q in range(2):
                    dve.wait_ge(mpv_done, NT * (q + 1))
                    note(dve.tensor_copy(tb[:, cols(0)], ps[:, OB, :]))
                    dve.tensor_copy(tb[0:MD, cols(1)], ps[0:MD, MX + q, :]).then_inc(mo_taken, 1)
                    if q == 0:
                        small_product("mtr0")
            if experts:
                for s in range(SLOTS):
                    blocks = expert_blocks(s) if token else []
                    for f, j in blocks[0:3]:
                        reduce_block(f, j)
                    if s % 2 == 1 and s >= 3:
                        u = (s - 3) // 2
                        e, h = u // 2, u % 2
                        dve.wait_ge(y_ready, u + 1)
                        if u >= 2:
                            dve.wait_ge(y_used, u - 1)
                            sync()
                        for t in range(4):
                            tt = 4 * h + t
                            ins = dve.scalar_tensor_tensor(out=toke[:, tt, :],
                                                           in0=ps[:, SC + 2 + u % 2, t * P:(t + 1) * P],
                                                           scalar=gate[:, tt, e:e + 1], in1=toke[:, tt, :],
                                                           op0=ALU.mult, op1=ALU.add)
                            if t < 3:
                                note(ins)
                        ins.then_inc(y_used, 1)
                    for f, j in blocks[3:]:
                        reduce_block(f, j)
                    if token:
                        if s == 14:
                            start_pre()
                        if s == 16:
                            start_x1()
                        if s == 17:
                            group_stats(x1, "norm")
                        if s == 19:
                            start_xh()
                        for name in EXPERT_WINDOW.get(s - 1, ()):
                            if name in ("kB", "qB"):
                                third_part_b(name)
                        for name in EXPERT_WINDOW.get(s, ()):
                            small_product(name)
            if front and not token:
                start_pre()
                small_product("pre")
                start_x1()
                group_stats(x1, "norm")
                small_product("norm")
                start_xh()
            if front:
                late = []
                for n in range(2 * STEPS):
                    names = [x for x in TOKEN_WINDOW.get(n, ()) if token or for_front(x)]
                    late_now = [x for x in names[-1:] if x != "turn_a0_2"]
                    attention_step(token_blocks(n, token), late, names[:len(names) - len(late_now)])
                    late = late_now

        def run_block(img, conv, experts, token, front, small):
            with nc.Block(no_gpsimd_drain=True) as block:
                @block.sync
                def _(sp):
                    sync_program(sp, img, conv, experts, token, front, small)

                @block.gpsimd
                def _(pool):
                    pool_program(pool, conv, experts, token, front, small)

                @block.tensor
                def _(pe):
                    tensor_program(pe, conv, experts, token, front, small)

                @block.scalar
                def _(act):
                    scalar_program(act, conv, experts, token, front, small)

                @block.vector
                def _(dve):
                    vector_program(dve, conv, experts, token, front, small)
            nc.all_engine_barrier(sems_to_clear=cleared)

        run_block(0, False, False, False, True, Small(START_WINDOW, only(TOKEN_WINDOW, for_front)))
        with nc.Fori(0, NB) as img:
            run_block(img, True, True, True, True, Small(CONV_WINDOW, PARTS_WINDOW, EXPERT_WINDOW, TOKEN_WINDOW))
        run_block(0, False, True, False, False, Small(only(CONV_WINDOW, for_last_norm)))


def kernel(**inputs):
    import numpy as np
    import concourse.bacc as bacc
    from concourse.bass_utils import run_bass_kernel_spmd

    g = {k: np.asarray(v) for k, v in inputs.items()}
    L0 = {k[len("L0_conv_"):]: v for k, v in g.items() if k.startswith("L0_conv_")}
    NB = g["x"].shape[0]
    f32 = np.float32

    eye = np.eye(P, dtype=f32)
    group = np.kron(np.eye(P // 4), np.full((4, 4), 0.25)).astype(f32)
    ff1 = L0["ff_w1"].T
    qkv = g["L1_attn_w_qkv"]
    table = {
        "wk": L0["wk"].T, "wq": L0["wq"].T, "wv": L0["wv"].T,
        "wqB": qkv[:, 0:P], "wkB": qkv[:, P:2 * P], "wvB": qkv[:, 2 * P:],
        "ffa": ff1[:P], "ffb": ff1[P:],
        "ff2": L0["ff_w2"].T, "out": L0["out_w"].T,
        "wvm": np.concatenate([L0["wv0"].T, L0["wv1"].T], 1),
        "wkm0": np.concatenate([L0["wk0"].T] * 2, 1), "wkm1": np.concatenate([L0["wk1"].T] * 2, 1),
        "wqm0": np.concatenate([L0["wq0"].T] * 2, 1), "wqm1": np.concatenate([L0["wq1"].T] * 2, 1),
        "ident": eye, "group": group, "ones": np.ones((P, P), f32),
    }

    def column(vals, at=(0,)):
        o = np.zeros(P, f32)
        for a in at:
            o[a:a + len(vals)] = vals
        return o

    vtable = {n: L0[n] for n in VECTORS if n in L0}
    vtable["sa_b1"] = column(L0["sa_b1"], (0, 32, 64))
    vtable["sa_b2"] = column(L0["sa_b2"])
    vtable["sa_b3"] = np.broadcast_to(L0["sa_b3"], (P,))
    vtable["neg_half"] = np.full(P, -0.5, f32)
    s1 = L0["sa_w1"].reshape(HD, P).T
    sa1 = np.zeros((P, 96), f32)
    sa2 = np.zeros((96, 3, HD), f32)
    for dx in range(3):
        sa1[:, 32 * dx:32 * dx + HD] = s1
        sa2[32 * dx:32 * dx + HD] = L0["sa_w2"][:, :, :, dx].transpose(1, 2, 0)
    arrays = {
        "x": g["x"].reshape(NB, P, S),
        "pos": L0["pos_emb"].reshape(P, S),
        "wts": np.stack([table[n] for n in WEIGHTS], 1),
        "vecs": np.stack([vtable[n] for n in VECTORS], 1),
        "sa1": sa1, "sa2": sa2,
        "sa3": np.pad(np.repeat(L0["sa_w3"].reshape(HD, 1), P, 1), ((0, 96 - HD), (0, 0))),
        "w1": g["L1_ffn_w1"].transpose(1, 0, 2),
        "b1": g["L1_ffn_b1"].reshape(NE, NC, P).transpose(2, 0, 1),
        "w2": g["L1_ffn_w2"].reshape(NE, NC, P, P).transpose(2, 0, 1, 3).reshape(P, NE, HID),
        "b2": np.pad(g["L1_ffn_b2"], ((0, 96 - NE), (0, 0))),
        "gw": g["L1_ffn_gate_w"],
        "gb": np.broadcast_to(g["L1_ffn_gate_b"], (P, NT, NE)),
        "iota": np.broadcast_to(np.arange(NE, dtype=f32), (P, NT, NE)),
    }
    nc = bacc.Bacc("TRN2", target_bir_lowering=False, num_devices=1)
    feed, args = {}, []
    for name, a in arrays.items():
        a = np.ascontiguousarray(a)
        feed[f"in_{name}"] = a
        args.append(nc.dram_tensor(f"in_{name}", a.shape, mybir.dt.from_np(a.dtype), kind="ExternalInput").ap())
    out = nc.dram_tensor("out_0", (NB, P, S), F32, kind="ExternalOutput").ap()
    build(nc, *args, out)
    r = run_bass_kernel_spmd(nc, [feed], core_ids=[0])
    return r.results[0]["out_0"].reshape(NB, P, SIDE, SIDE)
```
